# Optimizing a Trainium2 kernel written in Bass

```python
import numpy as np
import jax
import jax.numpy as jnp

def _softmax(x, axis=-1):
    return jax.nn.softmax(x, axis=axis)

def _gelu(x):
    return jax.nn.gelu(x, approximate=True)

def _silu(x):
    return jax.nn.silu(x)

def _sigmoid(x):
    return jax.nn.sigmoid(x)

def _layernorm(x, axis=-1, eps=1e-05):
    m = jnp.mean(x, axis=axis, keepdims=True)
    v = jnp.var(x, axis=axis, keepdims=True)
    return (x - m) / jnp.sqrt(v + eps)

def _scatter_add(tgt, idx, src, axis=0):
    return tgt.at[idx].add(src)

def _segment_sum(src, seg, n):
    return jax.ops.segment_sum(src, seg, n)
kernel_name = 'mk_prb_d1_jaxref_r8_1aa76d'

def setup_inputs(seed: int=0):
    np.random.seed(seed)
    _w = jnp.asarray

    def _L0_attn_setup():
        import jax, jax.numpy as jnp
        import numpy as np
        NUM_HEADS = 32
        NUM_KV_HEADS = 8
        HEAD_DIM = 128
        key = jax.random.key(seed)
        ks = jax.random.split(key, 5)
        B, S, H = (2, 256, 512)
        Dq = NUM_HEADS * HEAD_DIM
        Dkv = NUM_KV_HEADS * HEAD_DIM
        return {'hidden_states': jax.random.normal(ks[0], (B, S, H), jnp.float32), 'w_q': jax.random.normal(ks[1], (H, Dq), jnp.float32) * 0.02, 'w_k': jax.random.normal(ks[2], (H, Dkv), jnp.float32) * 0.02, 'w_v': jax.random.normal(ks[3], (H, Dkv), jnp.float32) * 0.02, 'w_o': jax.random.normal(ks[4], (Dq, H), jnp.float32) * 0.02}
    _L0_attn_in = _L0_attn_setup()

    def _L0_ffn_setup():
        import jax, jax.numpy as jnp
        import numpy as np
        TOP_K = 2
        key = jax.random.key(seed)
        k0, k1, k2 = jax.random.split(key, 3)
        B, S, D, H, E = (4, 256, 512, 512, 8)
        sc = 1.0 / np.sqrt(D).astype(np.float32)
        x = jax.random.normal(k0, (B, S, D), dtype=jnp.float32)
        W_gate = jax.random.normal(k1, (D, E), dtype=jnp.float32) * sc
        b_gate = jnp.zeros((E,), dtype=jnp.float32)
        W_e = jax.random.normal(k2, (E, D, H), dtype=jnp.float32) * sc
        b_e = jnp.zeros((E, H), dtype=jnp.float32)
        return {'x': x, 'W_gate': W_gate, 'b_gate': b_gate, 'W_e': W_e, 'b_e': b_e}
    _L0_ffn_in = _L0_ffn_setup()
    _d = {'L0_attn_hidden_states': _L0_attn_in['hidden_states'], 'L0_attn_w_q': _L0_attn_in['w_q'], 'L0_attn_w_k': _L0_attn_in['w_k'], 'L0_attn_w_v': _L0_attn_in['w_v'], 'L0_attn_w_o': _L0_attn_in['w_o'], 'L0_ffn_W_gate': _L0_ffn_in['W_gate'], 'L0_ffn_b_gate': _L0_ffn_in['b_gate'], 'L0_ffn_W_e': _L0_ffn_in['W_e'], 'L0_ffn_b_e': _L0_ffn_in['b_e']}
    _x0 = _d['L0_attn_hidden_states']
    _d['L0_attn_hidden_states'] = jax.random.normal(jax.random.fold_in(jax.random.key(seed), 1), (4, 512, 512), dtype=_x0.dtype)
    del _x0
    return _d

def reference(L0_attn_hidden_states, L0_attn_w_q, L0_attn_w_k, L0_attn_w_v, L0_attn_w_o, L0_ffn_W_gate, L0_ffn_b_gate, L0_ffn_W_e, L0_ffn_b_e):

    def _L0_attn_ref(hidden_states, w_q, w_k, w_v, w_o):
        import jax, jax.numpy as jnp
        import numpy as np
        NUM_HEADS = 32
        NUM_KV_HEADS = 8
        HEAD_DIM = 128
        B, S, _ = hidden_states.shape
        Hq, Hkv, D = (NUM_HEADS, NUM_KV_HEADS, HEAD_DIM)
        g = Hq // Hkv
        scale = D ** (-0.5)
        q = (hidden_states @ w_q).reshape(B, S, Hkv, g, D)
        k = (hidden_states @ w_k).reshape(B, S, Hkv, D)
        v = (hidden_states @ w_v).reshape(B, S, Hkv, D)
        scores = jnp.einsum('bqhgd,bkhd->bhgqk', q, k) * scale
        causal = jnp.tril(jnp.ones((S, S), dtype=bool))
        scores = jnp.where(causal, scores, -jnp.inf)
        probs = jax.nn.softmax(scores.astype(jnp.float32), axis=-1).astype(q.dtype)
        attn = jnp.einsum('bhgqk,bkhd->bqhgd', probs, v)
        attn = attn.reshape(B, S, Hq * D)
        return attn @ w_o

    def _L0_ffn_ref(x, W_gate, b_gate, W_e, b_e):
        import jax, jax.numpy as jnp
        import numpy as np
        TOP_K = 2
        logits = x @ W_gate + b_gate
        _, top_idx = jax.lax.top_k(logits, TOP_K)
        y_all = jax.nn.relu(jnp.einsum('bsd,edh->bseh', x, W_e) + b_e)
        y = jnp.take_along_axis(y_all, top_idx[..., None], axis=2)
        return y.mean(axis=2)
    x = L0_attn_hidden_states
    xn = _layernorm(x, axis=-1)
    x = x + _L0_attn_ref(xn, L0_attn_w_q, L0_attn_w_k, L0_attn_w_v, L0_attn_w_o) + _L0_ffn_ref(xn, L0_ffn_W_gate, L0_ffn_b_gate, L0_ffn_W_e, L0_ffn_b_e)
    return x

_drawn_inputs = setup_inputs


def setup_inputs(seed=0):
    import zlib

    import numpy as np

    out = dict(_drawn_inputs(seed))
    spreads = {'L0_ffn_b_gate': (0.0, 0.1), 'L0_ffn_b_e': (0.0, 0.1)}
    factors = {'L0_attn_w_q': 4.961, 'L0_attn_w_k': 4.986}
    for name, (base, spread) in spreads.items():
        noise = np.random.default_rng([zlib.crc32(name.encode()), seed]).standard_normal(out[name].shape)
        drawn = base * np.exp(spread * noise) if base else spread * noise
        out[name] = jnp.asarray(drawn.astype(out[name].dtype))
    for name, factor in factors.items():
        out[name] = (out[name] * factor).astype(out[name].dtype)
    return out
```

```python
from contextlib import ExitStack

import concourse.bass as bass
from concourse import mybir

ALU = mybir.AluOpType
ACT = mybir.ActivationFunctionType
AX_X = mybir.AxisListType.X
F32 = mybir.dt.float32
F16 = mybir.dt.float16
I32 = mybir.dt.int32
U32 = mybir.dt.uint32
ABSMAX = bass.bass_isa.ReduceOp.absmax

P = 128
HEAD = 128
EPS = 1e-5
MASKED = -3.0e38
LOWEST = -3.4e38
HI, LO = 0, 1
PARTS = ((HI, HI), (HI, LO), (LO, HI))


def attention_moe(nc, x, w_q, w_k, w_v, w_o, w_gate, b_gate, w_e, b_e, out):
    B, S, D = x.shape
    T = B * S
    NT = T // P
    KT = D // P
    NKV = w_k.shape[1] // HEAD
    NQ = w_q.shape[1] // HEAD
    R = NQ // NKV
    NE = w_gate.shape[1]
    QT = S // P
    NIT = NKV * B
    NH = NIT * R
    assert (P, KT, R, QT, B, NE) == (128, 4, 4, 4, 4, 8)

    SCORE_AT = {3: 0, 2: 512, 0: 896, 1: 1024}
    SCORE_FILLS = ((3,), (2, 0), (1,))
    CAUSAL = P * QT * (QT + 1) // 2
    PT_AT = {0: 0, 1: 512, 3: 896, 2: 1024}
    PT_FILL = 1024

    ctx = ExitStack()
    with ctx:
        def sb(name, shape, dt, where=ctx):
            return where.enter_context(nc.sbuf_tensor(name, shape, dt))

        def pb(name, shape, dt):
            return ctx.enter_context(nc.psum_tensor(name, shape, dt))

        def sem(name):
            return ctx.enter_context(nc.semaphore(name))

        acc = sb("acc", [P, NT, D], F32)
        xt = sb("xt", [P, 2, KT, T], F16)
        wst = sb("wst", [P, 1280], F32)
        wst_q = wst[:, 0:512].rearrange("p (k c) -> p k c", k=KT)
        wst_o = wst[:, 512:1024]
        wst_k = wst[:, 1024:1152]
        wst_v = wst[:, 1152:1280]
        wq = sb("wq", [P, 2 * R, 2, KT, HEAD], F16)
        wk = sb("wk", [P, 2, KT, 2, HEAD], F16)
        wv = sb("wv", [P, 2, KT, 2, HEAD], F16)
        wo = sb("wo", [P, 2 * R, 2, D], F16)
        ident = sb("ident", [P, P], F16)
        causal = sb("causal", [P, S], F32)
        wmax = sb("wmax", [P, 4, NE], F32)
        wmax4 = sb("wmax4", [P, 4], F32)
        wall4 = sb("wall4", [P, 4], F32)
        wpow = sb("wpow", [P, 4], F32)
        winv = sb("winv", [P, 4], F32)
        wscale = sb("wscale", [P, 4], F32)
        score_scale = sb("score_scale", [P, 1], F32)
        neg_score_scale = sb("neg_score_scale", [P, 1], F32)
        out_scale = sb("out_scale", [P, 1], F32)
        tmp1 = sb("tmp1", [P, 2], F32)

        early = ExitStack()
        xn = sb("xn", [P, 2, D], F32, early)
        xs = sb("xs", [P, 2, 2, D], F16, early)
        bn = sb("bn", [P, NT, 6], F32, early)
        mv = sb("mv", [P, NT, 2], F32, early)
        std = sb("std", [P, NT], F32, early)
        rstd = sb("rstd", [P, NT], F32, early)
        eps = sb("eps", [P, 1], F32, early)
        wg32 = sb("wg32", [P, KT, NE], F32, early)
        wg = sb("wg", [P, 2, KT, NE], F16, early)
        bg = sb("bg", [P, NE], F32, early)
        iota8 = sb("iota8", [P, NE], F32, early)
        logits = sb("logits", [P, NT, NE], F32, early)
        top8 = sb("top8", [P, NT, 8], F32, early)
        top8i = sb("top8i", [P, NT, 8], U32, early)
        top2 = sb("top2", [P, NT, 2], F32, early)
        is1 = sb("is1", [P, NT, NE], F32, early)
        is2 = sb("is2", [P, NT, NE], F32, early)
        half = sb("half", [P, NT, NE], F32, early)
        we32 = sb("we32", [P, KT, D], F32, early)
        we = sb("we", [P, 2, 2, KT, D], F16, early)
        be = sb("be", [P, NE, D], F32, early)
        emax = sb("emax", [P, NE + 1], F32, early)
        eall = sb("eall", [P, NE + 1], F32, early)
        epow = sb("epow", [P, NE + 1], F32, early)
        einv = sb("einv", [P, NE + 1], F32, early)
        escale = sb("escale", [P, NE + 1], F32, early)
        eundo = sb("eundo", [P, NE + 1], F32, early)
        pre = sb("pre", [P, 2, D], F32, early)
        act_y = sb("act_y", [P, 2, D], F32, early)
        scan = sb("scan", [P, 5120], F32, early)
        early.close()

        kT = sb("kT", [P, 2, S], F16)
        vs = sb("vs", [P, 2, QT, HEAD], F16)
        qT = sb("qT", [P, 2, 2, S], F16)
        pr = sb("pr", [P, 2, CAUSAL], F32)
        ps_split = sb("ps_split", [P, 2, 2, CAUSAL], F16)
        pT = sb("pT", [P, 2, 2, CAUSAL], F16)
        oT = sb("oT", [P, 2, R, 2, S], F16)
        carrier = sb("carrier", [P, 2, 3], F32)
        rowmax = sb("rowmax", [P, 2, QT], F32)
        negmax = sb("negmax", [P, 2, QT], F32)
        rowsum = sb("rowsum", [P, 2, QT], F32)
        rinv = sb("rinv", [P, 2, QT], F32)

        gen = [pb(f"gen{i}", [P, 512], F32) for i in range(2)]
        sco = [pb(f"sco{i}", [P, 512], F32) for i in range(2)]
        tra = [pb(f"tra{i}", [P, 1024], F16) for i in range(2)]
        att = [pb(f"att{i}", [P, 512], F32) for i in range(2)]
        ring4 = [sco[0], sco[1], att[0], att[1]]

        x_loaded = [sem(f"x_loaded{b}") for b in range(B)]
        gate_loaded = sem("gate_loaded")
        be_loaded = sem("be_loaded")
        we_loaded = sem("we_loaded")
        scan_loaded = sem("scan_loaded")
        w_loaded = sem("w_loaded")
        stored = sem("stored")
        consts = sem("consts")
        dve_chain = sem("dve_chain")
        std_done = sem("std_done")
        stats_done = sem("stats_done")
        xn_done = sem("xn_done")
        xhi_done = sem("xhi_done")
        xlo_done = sem("xlo_done")
        xt_filled = sem("xt_filled")
        xt_done = sem("xt_done")
        emax_done = sem("emax_done")
        eall_done = sem("eall_done")
        escale_done = sem("escale_done")
        wghi_done = sem("wghi_done")
        wg_done = sem("wg_done")
        gate_filled = sem("gate_filled")
        half_done = sem("half_done")
        wehi_done = sem("wehi_done")
        we_done = sem("we_done")
        y_filled = sem("y_filled")
        y_free = sem("y_free")
        relu_done = sem("relu_done")
        y_added = sem("y_added")
        scan_free = sem("scan_free")
        wmax_done = sem("wmax_done")
        wall_done = sem("wall_done")
        wscale_done = sem("wscale_done")
        w_hi = sem("w_hi")
        w_ready = sem("w_ready")
        q_filled, q_hi, q_ready = sem("q_filled"), sem("q_hi"), sem("q_ready")
        k_filled, k_hi, k_ready = sem("k_filled"), sem("k_hi"), sem("k_ready")
        v_filled, v_hi, v_ready = sem("v_filled"), sem("v_hi"), sem("v_ready")
        s_filled = sem("s_filled")
        s_masked = sem("s_masked")
        bias_ready = sem("bias_ready")
        exp_done = sem("exp_done")
        rinv_done = sem("rinv_done")
        p_hi = sem("p_hi")
        p_split = sem("p_split")
        pt_filled, pt_ready = sem("pt_filled"), sem("pt_ready")
        o_filled, o_hi, o_ready = sem("o_filled"), sem("o_hi"), sem("o_ready")
        out_filled, out_added = sem("out_filled"), sem("out_added")

        x_v = x.rearrange("b (t p) d -> b p t d", p=P)
        out_v = out.rearrange("b (t p) d -> b p t d", p=P)
        wq_v = w_q.rearrange("(k p) c -> p k c", p=P)
        wk_v = w_k.rearrange("(k p) c -> p k c", p=P)
        wv_v = w_v.rearrange("(k p) c -> p k c", p=P)
        wo_v = w_o.rearrange("(h p) n -> p h n", p=P)
        scan_v = [(w.rearrange("(p a) n -> p (a n)", p=P), w.shape[0] * w.shape[1] // P // NE)
                  for w in (w_q, w_k, w_v, w_o)]
        SCAN_AT = [sum(n for _, n in scan_v[:i]) for i in range(4)]

        def scanned(i):
            return scan[:, SCAN_AT[i]:SCAN_AT[i] + scan_v[i][1]]

        block = ctx.enter_context(nc.Block())

        @block.sync
        def _(sp):
            for b in range(B):
                sp.dma_start(acc[:, b * QT:(b + 1) * QT, :], x_v[b]).then_inc(x_loaded[b], 16)
                if b == 0:
                    sp.dma_start(wg32[:, :, :], w_gate.rearrange("(k p) e -> p k e", p=P)).then_inc(gate_loaded, 16)
                    sp.dma_start(bg[:, :], b_gate.partition_broadcast(P)).then_inc(gate_loaded, 16)
                    sp.dma_start(we32[:, :, :], w_e[0].rearrange("(k p) n -> p k n", p=P)).then_inc(we_loaded, 16)
            sp.dma_start(be[:, :, :], b_e.partition_broadcast(P)).then_inc(be_loaded, 16)

            with sp.Fori(0, NE) as e:
                sp.wait_ge(we_done, e + 1)
                sp.dma_start(we32[:, :, :],
                             w_e[bass.ds((e + 1) % NE, 1)].rearrange("e (k p) n -> p (e k) n", p=P)
                             ).then_inc(we_loaded, 16)
                sp.wait_ge(scan_free, e + 1)
                for i, (view, n) in enumerate(scan_v):
                    sp.dma_start(scanned(i), view[:, bass.ds(e * n, n)]).then_inc(scan_loaded, 16)

            def load_piece(j, o_too=True):
                h = j % NQ
                sp.dma_start(wst_q, wq_v[:, :, bass.ds(h * HEAD, HEAD)]).then_inc(w_loaded, 16)
                sp.dma_start(wst_k, wk_v[:, bass.ds(h % KT, 1), bass.ds((h // R) * HEAD, HEAD)]).then_inc(w_loaded, 16)
                sp.dma_start(wst_v, wv_v[:, bass.ds(h % KT, 1), bass.ds((h // R) * HEAD, HEAD)]).then_inc(w_loaded, 16)
                sp.dma_start(wst_o, wo_v[:, bass.ds((j + NQ - 2) % NQ, 1), :]).then_inc(w_loaded, 16)

            for j in range(5):
                if j:
                    sp.wait_ge(w_ready, j)
                load_piece(j)
            sp.wait_ge(w_ready, 5)
            load_piece(5)
            with sp.Fori(1, NIT - 1) as it:
                sp.wait_ge(w_ready, it + 5)
                load_piece(it + 5)
            for b in range(B - 1):
                sp.wait_ge(out_added, QT * (NIT - B + b + 1))
                sp.dma_start(out_v[b], acc[:, b * QT:(b + 1) * QT, :]).then_inc(stored, 16)
            for t in range(QT):
                sp.wait_ge(out_added, QT * (NIT - 1) + t + 1)
                sp.dma_start(out_v[B - 1][:, t, :], acc[:, (B - 1) * QT + t, :]).then_inc(stored, 16)
            sp.wait_ge(stored, 16 * (B - 1 + QT))

        @block.gpsimd
        def _(pool):
            pool.memset(ident[:, :], 0.0).then_inc(consts, 1)
            pool.memset(causal[:, :], 0.0).then_inc(consts, 1)
            pool.wait_ge(consts, 2)
            pool.affine_select(out=ident[:, :], in_=ident[:, :], compare_op=ALU.not_equal, fill=1.0, base=0,
                               pattern=[[-1, P]], channel_multiplier=1).then_inc(consts, 1)
            pool.affine_select(out=causal[:, S - P:S], in_=causal[:, S - P:S], compare_op=ALU.is_ge, fill=MASKED,
                               base=0, pattern=[[-1, P]], channel_multiplier=1).then_inc(consts, 1)
            pool.iota(iota8[:, :], pattern=[[1, NE]], base=0, channel_multiplier=0,
                      allow_small_or_imprecise_dtypes=True).then_inc(consts, 1)
            for e in range(NE + 1):
                pool.wait_ge(emax_done, e + 1)
                pool.partition_all_reduce(eall[:, :], emax[:, :], P, ABSMAX).then_inc(eall_done, 1)
            pool.wait_ge(wmax_done, 1)
            pool.partition_all_reduce(wall4[:, :], wmax4[:, :], P, ABSMAX).then_inc(wall_done, 1)

        @block.scalar
        def _(act):
            act.wait_ge(stats_done, 1)
            for b in range(B):
                act.wait_ge(stats_done, b + 2)
                act.activation(std[:, b * QT:(b + 1) * QT], mv[:, b * QT:(b + 1) * QT, 1], ACT.Sqrt,
                               bias=eps[:, 0:1]).then_inc(std_done, 1)
                for t in range(b * QT, (b + 1) * QT):
                    act.wait_ge(xn_done, t + 1)
                    if t >= 2:
                        act.wait_ge(xt_filled, t - 1)
                    act.activation(xs[:, t % 2, HI, :], xn[:, t % 2, :], ACT.Copy).then_inc(xhi_done, 1)
                    act.wait_ge(xt_filled, t + 1)
                    act.activation(xt[:, :, :, t * P:(t + 1) * P],
                                   tra[t % 2][:, :].rearrange("p (s k c) -> p s k c", s=2, k=KT),
                                   ACT.Copy).then_inc(xt_done, 1)
            act.wait_ge(escale_done, 1)
            act.activation(wg[:, HI], wg32[:, :, :], ACT.Copy, scale=escale[:, NE:NE + 1]).then_inc(wghi_done, 1)

            def expert_hi(e):
                act.activation(we[:, bass.ds(e % 2, 1), HI], we32[:, :, :], ACT.Copy,
                               scale=escale[:, bass.ds(e % NE, 1)]).then_inc(wehi_done, 1)

            expert_hi(0)
            act.wait_ge(half_done, 1)
            with act.Fori(0, NE) as e:
                for t in range(NT):
                    act.wait_ge(y_free, NT * e + t + 1 + 4)
                    if t >= 2:
                        act.wait_ge(y_added, NT * e + t - 1)
                    act.activation(act_y[:, t % 2, :], pre[:, t % 2, :], ACT.Relu,
                                   scale=half[:, t, bass.ds(e, 1)]).then_inc(relu_done, 1)
                    if t == 3:
                        act.wait_ge(escale_done, e + 2)
                        expert_hi(e + 1)

            act.wait_ge(wscale_done, 1)

            def weights_hi(j):
                act.wait_ge(w_loaded, 64 * j + 64)
                act.activation(wq[:, bass.ds(j % (2 * R), 1), HI], wst_q, ACT.Copy, scale=wscale[:, 0:1])
                act.activation(wk[:, bass.ds((j // R) % 2, 1), bass.ds(j % KT, 1), HI], wst_k, ACT.Copy,
                               scale=wscale[:, 1:2])
                act.activation(wv[:, bass.ds((j // R) % 2, 1), bass.ds(j % KT, 1), HI], wst_v, ACT.Copy,
                               scale=wscale[:, 2:3])
                act.activation(wo[:, bass.ds((j + 2 * R - 2) % (2 * R), 1), HI], wst_o, ACT.Copy,
                               scale=wscale[:, 3:4]).then_inc(w_hi, 1)

            def q_high(bank, h, slot):
                act.wait_ge(q_filled, h + 1)
                act.activation(qT[:, slot, HI, :], gen[bank][:, :], ACT.Copy).then_inc(q_hi, 1)

            def k_high(bank, it):
                act.wait_ge(k_filled, it + 1)
                act.activation(kT[:, HI, :], gen[bank][:, :], ACT.Copy).then_inc(k_hi, 1)

            def v_high(bank, it):
                act.wait_ge(v_filled, it + 1)
                act.activation(vs[:, HI], gen[bank][:, :].rearrange("p (t d) -> p t d", t=QT),
                               ACT.Copy).then_inc(v_hi, 1)

            def exps(h, slot):
                act.wait_ge(bias_ready, h + 1)
                for i in range(QT):
                    a = SCORE_AT[i]
                    row = pr[:, slot, a:a + P * (i + 1)]
                    last = act.activation(row, row, ACT.Exp, bias=negmax[:, slot, i:i + 1],
                                          scale=score_scale[:, 0:1], accum_out=rowsum[:, slot, i:i + 1])
                last.then_inc(exp_done, 1)

            def pt_copies(h, slot, fills):
                for u in fills:
                    act.wait_ge(pt_filled, 3 * h + u + 1)
                    bank = tra[(3 * slot + u) % 2]
                    if u < 2:
                        src, dst = bank[:, :], pT[:, slot, u, 0:PT_FILL]
                    else:
                        w = CAUSAL - PT_FILL
                        src, dst = bank[:, 0:2 * w].rearrange("p (s c) -> p s c", s=2), pT[:, slot, :, PT_FILL:CAUSAL]
                    act.activation(dst, src, ACT.Copy).then_inc(pt_ready, 1)

            def o_high(h, it, r):
                act.wait_ge(o_filled, h + 1)
                act.activation(oT[:, bass.ds(it % 2, 1), r, HI, :], att[r % 2][:, :], ACT.Copy).then_inc(o_hi, 1)

            for j in range(5):
                if j:
                    act.wait_ge(w_ready, j)
                weights_hi(j)
            k_high(0, 0)
            for h in range(3):
                q_high((1, 0, 1)[h], h, h % 2)
                if h < 2:
                    exps(h, h)

            def pair(it, first=False, last=False):
                for r in range(R):
                    n = it * R + r
                    if r != 3 and not (last and r >= 1):
                        q_high(Q_BANK[r], n + 3, (r + 1) % 2)
                    pt_copies(n, r % 2, (0, 1))
                    if r == 1 and not last:
                        k_high(1, it + 1)
                    if r == 3 and not last:
                        q_high(Q_BANK[r], n + 3, (r + 1) % 2)
                    if not (first and r == 0):
                        o_high(n - 1, it if r else it - 1, (r - 1) % R)
                    pt_copies(n, r % 2, (2,))
                    if not (last and r >= 2):
                        exps(n + 2, r % 2)
                    if r == 0:
                        v_high(1, it)
                    if r == 2 and not last:
                        act.wait_ge(k_filled, it + 2)
                        weights_hi(it + 5)

            pair(0, first=True)
            with act.Fori(1, NIT - 1) as it:
                pair(it)
            pair(NIT - 1, last=True)
            o_high(NH - 1, NIT - 1, R - 1)

        @block.vector
        def _(dve):
            chain = [0]

            def link(ins):
                chain[0] += 1
                ins.then_inc(dve_chain, 1)
                dve.wait_ge(dve_chain, chain[0])

            def powers(allmax, pow2, inv, scale):
                link(dve.tensor_scalar(pow2, allmax, 2.0 ** -60, None, ALU.max))
                link(dve.tensor_scalar(pow2.bitcast(I32), pow2.bitcast(I32), 0x7F800000, None, ALU.bitwise_and))
                link(dve.reciprocal(inv, pow2))
                return dve.tensor_scalar(scale, inv, 8.0, None, ALU.mult)

            dve.memset(eps[:, :], EPS).then_inc(stats_done, 1)
            link(dve.memset(emax[:, :], 0.0))
            dve.memset(tmp1[:, 1:2], 0.0).then_inc(scan_free, 1)

            for b in range(B):
                tiles = range(b * QT, (b + 1) * QT)
                dve.wait_ge(x_loaded[b], 16)
                for t in tiles:
                    ins = dve.bn_stats(bn[:, t, :], acc[:, t, :])
                link(ins)
                for t in tiles:
                    ins = dve.bn_aggr(mv[:, t, :], bn[:, t, :])
                ins.then_inc(stats_done, 1)
                if b == 0:
                    dve.wait_ge(gate_loaded, 32)
                    dve.tensor_reduce(emax[:, NE:NE + 1], wg32[:, :, :], mybir.AxisListType.XY, ALU.max,
                                      apply_absolute_value=True)
                    dve.wait_ge(we_loaded, 16)
                    dve.tensor_reduce(emax[:, 0:1], we32[:, :, :], mybir.AxisListType.XY, ALU.max,
                                      apply_absolute_value=True).then_inc(emax_done, 1)
                dve.wait_ge(std_done, b + 1)
                link(dve.reciprocal(rstd[:, b * QT:(b + 1) * QT], std[:, b * QT:(b + 1) * QT]))
                for t in tiles:
                    if t >= 2:
                        dve.wait_ge(xhi_done, t - 1)
                    dve.tensor_scalar(xn[:, t % 2, :], acc[:, t, :], mv[:, t, 0:1], rstd[:, t:t + 1],
                                      ALU.subtract, ALU.mult).then_inc(xn_done, 1)
                    dve.wait_ge(xhi_done, t + 1)
                    dve.wait_ge(xn_done, t + 1)
                    if t >= 2:
                        dve.wait_ge(xt_filled, t - 1)
                    dve.tensor_tensor(xs[:, t % 2, LO, :], xn[:, t % 2, :], xs[:, t % 2, HI, :],
                                      ALU.subtract).then_inc(xlo_done, 1)

            dve.wait_ge(eall_done, 1)
            link(powers(eall[:, NE:NE + 1], epow[:, NE:NE + 1], einv[:, NE:NE + 1], escale[:, NE:NE + 1]))
            powers(eall[:, 0:1], epow[:, 0:1], einv[:, 0:1], escale[:, 0:1]).then_inc(escale_done, 1)
            link(dve.tensor_scalar(eundo[:, 0:1], epow[:, 0:1], 0.125, None, ALU.mult))
            link(dve.tensor_scalar(eundo[:, NE:NE + 1], epow[:, NE:NE + 1], 0.125, None, ALU.mult))
            dve.wait_ge(escale_done, 1)
            dve.wait_ge(wghi_done, 1)
            dve.scalar_tensor_tensor(out=wg[:, LO], in0=wg32[:, :, :], scalar=escale[:, NE:NE + 1], in1=wg[:, HI],
                                     op0=ALU.mult, op1=ALU.subtract).then_inc(wg_done, 1)

            def expert_lo(e):
                dve.wait_ge(wehi_done, e + 1)
                dve.scalar_tensor_tensor(out=we[:, bass.ds(e % 2, 1), LO].rearrange("p e k n -> p (e k n)"),
                                         in0=we32[:, :, :].rearrange("p k n -> p (k n)"),
                                         scalar=escale[:, bass.ds(e % NE, 1)],
                                         in1=we[:, bass.ds(e % 2, 1), HI].rearrange("p e k n -> p (e k n)"),
                                         op0=ALU.mult, op1=ALU.subtract).then_inc(we_done, 1)

            expert_lo(0)
            dve.wait_ge(gate_filled, 1)
            for t in range(NT):
                ins = dve.scalar_tensor_tensor(out=logits[:, t, :], in0=gen[0][:, t * NE:(t + 1) * NE],
                                               scalar=eundo[:, NE:NE + 1], in1=bg[:, :], op0=ALU.mult, op1=ALU.add)
            link(ins)
            for t in range(NT):
                ins = dve.max(top8[:, t, :], logits[:, t, :])
            link(ins)
            for t in range(NT):
                ins = dve.max_index(top8i[:, t, :], top8[:, t, :], logits[:, t, :])
            link(ins)
            link(dve.tensor_copy(top2[:, :, :], top8i[:, :, 0:2]))
            dve.wait_ge(consts, 5)
            all_iota = iota8[:, :].unsqueeze(1).broadcast_to([P, NT, NE])
            dve.tensor_tensor(is1[:, :, :], all_iota, top2[:, :, 0:1].broadcast_to([P, NT, NE]), ALU.is_equal)
            link(dve.tensor_tensor(is2[:, :, :], all_iota, top2[:, :, 1:2].broadcast_to([P, NT, NE]), ALU.is_equal))
            link(dve.tensor_tensor(is1[:, :, :], is1[:, :, :], is2[:, :, :], ALU.add))
            dve.tensor_scalar(half[:, :, :], is1[:, :, :], 0.5, None, ALU.mult).then_inc(half_done, 1)

            dve.wait_ge(be_loaded, 16)
            dve.memset(tmp1[:, :], 0.0).then_inc(y_free, 4)

            def add_y(e, t):
                dve.wait_ge(relu_done, NT * e + t + 1)
                dve.tensor_tensor(acc[:, t, :], acc[:, t, :], act_y[:, t % 2, :], ALU.add).then_inc(y_added, 1)

            sub = chain[0]
            CH = 4
            with dve.Fori(0, NE) as e:
                step = [0]

                def elink(ins):
                    step[0] += 1
                    ins.then_inc(dve_chain, 1)
                    dve.wait_ge(dve_chain, sub + CH * e + step[0])

                nxt = bass.ds((e + 1) % NE, 1)
                dve.wait_ge(we_loaded, 16 * (e + 2))
                dve.tensor_reduce(emax[:, nxt], we32[:, :, :].rearrange("p k n -> p (k n)"), AX_X, ALU.max,
                                  apply_absolute_value=True).then_inc(emax_done, 1)
                for t in range(NT):
                    dve.wait_ge(y_filled, NT * e + t + 1)
                    if t >= 2:
                        dve.wait_ge(relu_done, NT * e + t - 1)
                    dve.scalar_tensor_tensor(out=pre[:, t % 2, :], in0=ring4[t % 4][:, :],
                                             scalar=eundo[:, bass.ds(e, 1)], in1=be[:, bass.ds(e, 1), :],
                                             op0=ALU.mult, op1=ALU.add).then_inc(y_free, 1)
                    if t >= 1:
                        add_y(e, t - 1)
                    if t == 2:
                        dve.wait_ge(eall_done, e + 2)
                        elink(dve.tensor_scalar(epow[:, nxt], eall[:, nxt], 2.0 ** -60, None, ALU.max))
                        elink(dve.tensor_scalar(epow[:, nxt].bitcast(I32), epow[:, nxt].bitcast(I32), 0x7F800000,
                                                None, ALU.bitwise_and))
                        elink(dve.reciprocal(einv[:, nxt], epow[:, nxt]))
                        elink(dve.tensor_scalar(escale[:, nxt], einv[:, nxt], 8.0, None, ALU.mult))
                        dve.tensor_scalar(eundo[:, nxt], epow[:, nxt], 0.125, None, ALU.mult).then_inc(escale_done, 1)
                    if t == 5:
                        expert_lo(e + 1)
                    if t == 8:
                        dve.wait_ge(scan_loaded, 64 * (e + 1))
                        for i in range(3):
                            dve.tensor_reduce(wmax[:, i, bass.ds(e, 1)], scanned(i), AX_X, ALU.max,
                                              apply_absolute_value=True)
                    if t == 11:
                        dve.tensor_reduce(wmax[:, 3, bass.ds(e, 1)], scanned(3), AX_X, ALU.max,
                                          apply_absolute_value=True).then_inc(scan_free, 1)
                add_y(e, NT - 1)
                assert step[0] == CH
            chain[0] = sub + CH * NE

            dve.wait_ge(scan_free, NE + 1)
            dve.tensor_reduce(wmax4[:, :], wmax[:, :, :], AX_X, ALU.max).then_inc(wmax_done, 1)
            dve.wait_ge(wall_done, 1)
            link(powers(wall4[:, :], wpow[:, :], winv[:, :], wscale[:, :]))
            link(dve.tensor_scalar(tmp1[:, 0:1], wpow[:, 0:1], wpow[:, 1:2], HEAD ** -0.5 / 64, ALU.mult, ALU.mult))
            dve.tensor_copy(score_scale[:, :], tmp1[:, 0:1])
            dve.tensor_scalar(neg_score_scale[:, :], tmp1[:, 0:1], -1.0, None, ALU.mult)
            link(dve.tensor_scalar(out_scale[:, :], wpow[:, 2:3], wpow[:, 3:4], 1.0 / 64, ALU.mult, ALU.mult))
            dve.tensor_copy(tmp1[:, 0:1], out_scale[:, :]).then_inc(wscale_done, 1)

            def weights_lo(j):
                dve.wait_ge(w_hi, j + 1)

                def low(dst, src, high, m):
                    return dve.scalar_tensor_tensor(out=dst, in0=src, scalar=wscale[:, m:m + 1], in1=high,
                                                    op0=ALU.mult, op1=ALU.subtract)

                q = wq[:, bass.ds(j % (2 * R), 1)]
                low(q[:, :, LO].rearrange("p e k c -> p (e k c)"), wst[:, 0:512],
                    q[:, :, HI].rearrange("p e k c -> p (e k c)"), 0)
                for w, src, m in ((wk, wst_k, 1), (wv, wst_v, 2)):
                    a = w[:, bass.ds((j // R) % 2, 1), bass.ds(j % KT, 1)]
                    low(a[:, :, :, LO].rearrange("p a b c -> p (a b c)"), src,
                        a[:, :, :, HI].rearrange("p a b c -> p (a b c)"), m)
                o = wo[:, bass.ds((j + 2 * R - 2) % (2 * R), 1)]
                low(o[:, :, LO].rearrange("p e n -> p (e n)"), wst_o,
                    o[:, :, HI].rearrange("p e n -> p (e n)"), 3).then_inc(w_ready, 1)

            def mask_rows(h, slot, fills=(0, 1, 2)):
                if not (isinstance(h, int) and h < 2) and 0 in fills:
                    dve.wait_ge(p_split, h - 1)
                for u in fills:
                    tiles = SCORE_FILLS[u]
                    dve.wait_ge(s_filled, 3 * h + u + 1)
                    dve.memset(carrier[:, slot, u:u + 1], 0.0)
                    at = 0
                    for i in tiles:
                        w = P * (i + 1)
                        a = SCORE_AT[i]
                        ins = dve.tensor_tensor_reduce(pr[:, slot, a:a + w], sco[(3 * slot + u) % 2][:, at:at + w],
                                                       causal[:, S - w:S], 1.0, LOWEST, ALU.add, ALU.max,
                                                       rowmax[:, slot, i:i + 1])
                        at += w
                    ins.then_inc(s_masked, 1)
                if 2 not in fills:
                    return
                dve.wait_ge(s_masked, 3 * h + 3)
                dve.tensor_scalar(negmax[:, slot, :], rowmax[:, slot, :], neg_score_scale[:, 0:1], None,
                                  ALU.mult).then_inc(bias_ready, 1)

            def split_hi(h, slot):
                dve.wait_ge(exp_done, h + 1)
                dve.reciprocal(rinv[:, slot, :], rowsum[:, slot, :]).then_inc(rinv_done, 1)
                if not (isinstance(h, int) and h < 2):
                    dve.wait_ge(pt_filled, 3 * h - 3)
                dve.wait_ge(rinv_done, h + 1)
                for i in range(QT):
                    a, w = SCORE_AT[i], P * (i + 1)
                    ins = dve.tensor_scalar(ps_split[:, slot, HI, a:a + w], pr[:, slot, a:a + w],
                                            rinv[:, slot, i:i + 1], None, ALU.mult)
                ins.then_inc(p_hi, 1)

            def split_lo(h, slot):
                dve.wait_ge(p_hi, h + 1)
                for i in range(QT):
                    a, w = SCORE_AT[i], P * (i + 1)
                    ins = dve.scalar_tensor_tensor(out=ps_split[:, slot, LO, a:a + w], in0=pr[:, slot, a:a + w],
                                                   scalar=rinv[:, slot, i:i + 1], in1=ps_split[:, slot, HI, a:a + w],
                                                   op0=ALU.mult, op1=ALU.subtract)
                ins.then_inc(p_split, 1)

            def q_low(bank, h, slot):
                dve.wait_ge(q_hi, h + 1)
                dve.tensor_tensor(qT[:, slot, LO, :], gen[bank][:, :], qT[:, slot, HI, :],
                                  ALU.subtract).then_inc(q_ready, 1)

            def k_low(bank, it):
                dve.wait_ge(k_hi, it + 1)
                dve.tensor_tensor(kT[:, LO, :], gen[bank][:, :], kT[:, HI, :], ALU.subtract).then_inc(k_ready, 1)

            def v_low(bank, it):
                dve.wait_ge(v_hi, it + 1)
                dve.tensor_tensor(vs[:, LO].rearrange("p t d -> p (t d)"), gen[bank][:, :],
                                  vs[:, HI].rearrange("p t d -> p (t d)"), ALU.subtract).then_inc(v_ready, 1)

            def o_low(h, it, r):
                dve.wait_ge(o_hi, h + 1)
                o = oT[:, bass.ds(it % 2, 1), r]
                dve.tensor_tensor(o[:, :, LO], att[r % 2][:, :].unsqueeze(1), o[:, :, HI], ALU.subtract).then_inc(o_ready, 1)

            def add_out(bank, it, t):
                dve.wait_ge(out_filled, QT * it + t + 1)
                a = acc[:, bass.ds((it % B) * QT + t, 1), :].rearrange("p e n -> p (e n)")
                dve.scalar_tensor_tensor(out=a, in0=gen[bank][:, :], scalar=out_scale[:, 0:1], in1=a,
                                         op0=ALU.mult, op1=ALU.add).then_inc(out_added, 1)

            for j in range(5):
                weights_lo(j)
            k_low(0, 0)
            for h in range(3):
                q_low((1, 0, 1)[h], h, h % 2)
                if h < 2:
                    mask_rows(h, h)
            split_hi(0, 0)
            split_lo(0, 0)

            def pair(it, first=False, last=False):
                for r in range(R):
                    n = it * R + r
                    scores = not (last and r >= 2)
                    more = not (last and r == R - 1)
                    if scores:
                        mask_rows(n + 2, r % 2, (0, 1))
                    if more:
                        split_hi(n + 1, (r + 1) % 2)
                    if r == 3 and not first:
                        add_out(OUT_BANK[2], it - 1, 2)
                    if r != 3 and not (last and r >= 1):
                        q_low(Q_BANK[r], n + 3, (r + 1) % 2)
                    if scores:
                        mask_rows(n + 2, r % 2, (2,))
                    if more:
                        split_lo(n + 1, (r + 1) % 2)
                    if r == 1 and not last:
                        k_low(1, it + 1)
                    if r == 3 and not last:
                        q_low(Q_BANK[r], n + 3, (r + 1) % 2)
                    if not (first and r == 0):
                        o_low(n - 1, it if r else it - 1, (r - 1) % R)
                    if r == 0:
                        v_low(1, it)
                    if r == 1 and not first:
                        add_out(OUT_BANK[0], it - 1, 0)
                    if r == 2 and not first:
                        add_out(OUT_BANK[1], it - 1, 1)
                    if r == 3 and not last:
                        weights_lo(it + 5)
                    if r == 3 and not first:
                        add_out(OUT_BANK[3], it - 1, 3)

            pair(0, first=True)
            with dve.Fori(1, NIT - 1) as it:
                pair(it)
            pair(NIT - 1, last=True)
            o_low(NH - 1, NIT - 1, R - 1)
            for t in range(QT):
                add_out(t % 2, NIT - 1, t)

        @block.tensor
        def _(pe):
            def products(dst, pairs):
                n = len(pairs)
                for i, (stat, mov) in enumerate(pairs):
                    for m, (a, b) in enumerate(PARTS):
                        ins = pe.matmul(dst, stat(a), mov(b), start=(i == 0 and m == 0),
                                        stop=(i == n - 1 and m == len(PARTS) - 1))
                return ins

            pe.wait_ge(consts, 5)
            for t in range(NT):
                pe.wait_ge(xhi_done, t + 1)
                pe.wait_ge(xlo_done, t + 1)
                if t >= 2:
                    pe.wait_ge(xt_done, t - 1)
                for s in (HI, LO):
                    for k in range(KT):
                        c = (s * KT + k) * P
                        ins = pe.transpose(tra[t % 2][:, c:c + P], xs[:, t % 2, s, k * P:(k + 1) * P], ident[:, :])
                ins.then_inc(xt_filled, 1)

            pe.wait_ge(wg_done, 1)
            pe.wait_ge(xt_done, NT)
            for t in range(NT):
                for k in range(KT):
                    for a in (HI, LO):
                        for b in (HI, LO):
                            ins = pe.matmul(gen[0][:, t * NE:(t + 1) * NE], xt[:, a, k, t * P:(t + 1) * P], wg[:, b, k, :],
                                            start=(k == 0 and a == HI and b == HI),
                                            stop=(k == KT - 1 and a == LO and b == LO))
            ins.then_inc(gate_filled, 1)

            with pe.Fori(0, NE) as e:
                pe.wait_ge(we_done, e + 1)
                for t in range(NT):
                    pe.wait_ge(y_free, NT * e + t + 1)
                    products(ring4[t % 4][:, :],
                             [(lambda a, k=k: xt[:, a, k, t * P:(t + 1) * P],
                               lambda b, k=k: we[:, bass.ds(e % 2, 1), b, k, :]) for k in range(KT)]).then_inc(y_filled, 1)

            def tokens(part, k, it, lo=0, n=S):
                return xt[:, part, k, bass.ds((it % B) * S + lo, n)]

            def fill_q(bank, h, it, r):
                w = bass.ds(((it // B) % 2) * R + r, 1)
                products(gen[bank][:, :], [(lambda a, k=k: wq[:, w, a, k, :], lambda b, k=k: tokens(b, k, it))
                                           for k in range(KT)]).then_inc(q_filled, 1)

            def fill_k(bank, it):
                w = bass.ds((it // B) % 2, 1)
                products(gen[bank][:, :], [(lambda a, k=k: wk[:, w, k, a, :], lambda b, k=k: tokens(b, k, it))
                                           for k in range(KT)]).then_inc(k_filled, 1)

            def fill_v(bank, it):
                w = bass.ds((it // B) % 2, 1)
                for t in range(QT):
                    ins = products(gen[bank][:, t * HEAD:(t + 1) * HEAD],
                                   [(lambda a, k=k: tokens(a, k, it, t * P, P), lambda b, k=k: wv[:, w, k, b, :])
                                    for k in range(KT)])
                ins.then_inc(v_filled, 1)

            def fill_scores(h, slot, fills=(0, 1, 2)):
                if 0 in fills:
                    pe.wait_ge(q_ready, h + 1)
                for u in fills:
                    tiles = SCORE_FILLS[u]
                    if not (isinstance(h, int) and 3 * h + u < 2):
                        pe.wait_ge(s_masked, 3 * h + u - 1)
                    at = 0
                    for i in tiles:
                        w = P * (i + 1)
                        ins = products(sco[(3 * slot + u) % 2][:, at:at + w],
                                       [(lambda a: qT[:, slot, a, i * P:(i + 1) * P], lambda b: kT[:, b, 0:w])])
                        at += w
                    ins.then_inc(s_filled, 1)

            def transpose_p(h, slot, fills):
                if 0 in fills:
                    pe.wait_ge(p_split, h + 1)
                for u in fills:
                    if not (isinstance(h, int) and 3 * h + u < 2):
                        pe.wait_ge(pt_ready, 3 * h + u - 1)
                    for part, j in ((u, 0), (u, 1), (u, 3)) if u < 2 else ((HI, 2), (LO, 2)):
                        for i in range(j, QT):
                            a = SCORE_AT[i] + j * P
                            c = PT_AT[j] % PT_FILL + (i - j) * P + (part * 2 * P if u == 2 else 0)
                            ins = pe.transpose(tra[(3 * slot + u) % 2][:, c:c + P], ps_split[:, slot, part, a:a + P],
                                               ident[:, :])
                    ins.then_inc(pt_filled, 1)

            def fill_o(h, slot):
                pe.wait_ge(pt_ready, 3 * h + 3)
                if not (isinstance(h, int) and h < 2):
                    pe.wait_ge(o_ready, h - 1)
                for j in range(QT):
                    w = S - j * P
                    for m, (a, b) in enumerate(PARTS):
                        ins = pe.matmul(att[slot][:, j * P:S], vs[:, a, j, :], pT[:, slot, b, PT_AT[j]:PT_AT[j] + w],
                                        start=(j == 0 and m == 0), stop=(j == QT - 1 and m == len(PARTS) - 1))
                ins.then_inc(o_filled, 1)

            def fill_out(bank, it, t):
                if t == 0:
                    pe.wait_ge(o_ready, R * it + R)
                w = (it // B) % 2
                products(gen[bank][:, :],
                         [(lambda a, r=r: oT[:, bass.ds(it % 2, 1), r, a, t * P:(t + 1) * P],
                           lambda b, r=r: wo[:, bass.ds(w * R + r, 1), b, :]) for r in range(R)]).then_inc(out_filled, 1)

            pe.wait_ge(y_free, NE * NT + 4)
            pe.wait_ge(w_ready, 5)
            fill_k(0, 0)
            fill_q(1, 0, 0, 0)
            pe.wait_ge(k_ready, 1)
            fill_q(0, 1, 0, 1)
            fill_scores(0, 0)
            fill_q(1, 2, 0, 2)
            fill_scores(1, 1)

            def pair(it, first=False, last=False):
                for r in range(R):
                    n = it * R + r
                    if r == 2 and not last:
                        pe.wait_ge(k_ready, it + 2)
                    if not (last and r >= 2):
                        fill_scores(n + 2, r % 2, (0, 1))
                    if r == 1:
                        pe.wait_ge(w_ready, NIT + 4 if last else it + 5)
                    if r == 3 and not first:
                        if last:
                            pe.wait_ge(v_ready, NIT)
                        else:
                            pe.wait_ge(q_ready, n + 3)
                        fill_out(1, it - 1, 2)
                    if r != 3 and not (last and r >= 1):
                        if r == 2:
                            pe.wait_ge(k_ready, it + 2)
                        else:
                            pe.wait_ge(q_ready, n + 3)
                        fill_q(Q_BANK[r], n + 3, it + (r > 0), (r + 3) % R)
                    if not (last and r >= 2):
                        fill_scores(n + 2, r % 2, (2,))
                    transpose_p(n, r % 2, (0, 1))
                    if r == 1 and not last:
                        pe.wait_ge(v_ready, it + 1)
                        fill_k(1, it + 1)
                    if r == 3 and not last:
                        if first:
                            pe.wait_ge(q_ready, n + 2)
                        else:
                            pe.wait_ge(out_added, QT * (it - 1) + 2)
                        fill_q(Q_BANK[r], n + 3, it + 1, (r + 3) % R)
                    if not (first and r == 0):
                        if r == 1:
                            pe.wait_ge(v_ready, it + 1)
                        fill_o(n - 1, (r + 1) % 2)
                    transpose_p(n, r % 2, (2,))
                    if r == 0:
                        if first:
                            pe.wait_ge(q_ready, 3)
                        else:
                            pe.wait_ge(q_ready, n + 4)
                        fill_v(1, it)
                    if r == 1 and not first:
                        pe.wait_ge(q_ready, NH if last else n + 4)
                        fill_out(0, it - 1, 0)
                    if r == 2 and not first:
                        pe.wait_ge(out_added, QT * (it - 1) + 1)
                        fill_out(0, it - 1, 1)
                    if r == 3 and not first:
                        pe.wait_ge(out_added, QT * (it - 1) + 3)
                        fill_out(1, it - 1, 3)

            pair(0, first=True)
            with pe.Fori(1, NIT - 1) as it:
                pair(it)
            pair(NIT - 1, last=True)
            fill_o(NH - 1, 1)
            for t in range(QT):
                pe.wait_ge(out_added, QT * (NIT - 1) + t - 1)
                fill_out(t % 2, NIT - 1, t)


Q_BANK = (0, 0, 1, 0)
OUT_BANK = (0, 0, 1, 1)


_INS = ['L0_attn_hidden_states', 'L0_attn_w_q', 'L0_attn_w_k', 'L0_attn_w_v', 'L0_attn_w_o', 'L0_ffn_W_gate',
        'L0_ffn_b_gate', 'L0_ffn_W_e', 'L0_ffn_b_e']


def kernel(**inputs):
    import numpy as _np
    import concourse.bacc as _bacc
    from concourse import mybir as _mybir
    from concourse.bass_utils import run_bass_kernel_spmd as _run

    nc = _bacc.Bacc("TRN2", target_bir_lowering=False, num_devices=1)
    arrays, args = {}, []
    for name in _INS:
        a = _np.ascontiguousarray(inputs[name])
        arrays[f"in_{name}_dram"] = a
        args.append(nc.dram_tensor(f"in_{name}_dram", a.shape, _mybir.dt.from_np(a.dtype), kind="ExternalInput").ap())
    shape = inputs[_INS[0]].shape
    args.append(nc.dram_tensor("out_0_dram", shape, F32, kind="ExternalOutput").ap())
    attention_moe(nc, *args)
    r = _run(nc, [arrays], core_ids=[0])
    return r.results[0]["out_0_dram"]
```

```python
from contextlib import ExitStack

import concourse.bass as bass
from concourse import mybir

ALU = mybir.AluOpType
ACT = mybir.ActivationFunctionType
AX_X = mybir.AxisListType.X
F32 = mybir.dt.float32
F16 = mybir.dt.float16
I32 = mybir.dt.int32
U32 = mybir.dt.uint32
ABSMAX = bass.bass_isa.ReduceOp.absmax

P = 128
HEAD = 128
EPS = 1e-5
MASKED = -3.0e38
LOWEST = -3.4e38
TOP = 2
HI, LO = 0, 1
PARTS = ((HI, HI), (HI, LO), (LO, HI))


def attention_moe(nc, x, w_q, w_k, w_v, w_o, w_gate, b_gate, w_e, b_e, out):
    B, S, D = x.shape
    T = B * S
    NT = T // P
    KT = D // P
    NKV = w_k.shape[1] // HEAD
    NQ = w_q.shape[1] // HEAD
    R = NQ // NKV
    NE = w_gate.shape[1]
    QT = S // P
    NIT = NKV * B
    NH = NIT * R
    NS = (TOP * T + NE * (P - 1)) // P
    RING = 3
    SCANS = 16
    EARLY_SCANS = 4
    assert (P, KT, R, QT, B, NE, NS % RING, NS // RING - 1 + EARLY_SCANS) == (128, 4, 4, 4, 4, 8, 0, SCANS)

    SCORE_AT = [P * i * (i + 1) // 2 for i in range(QT)]
    SCORE_FILLS = ((3,), (2, 0), (1,))
    CAUSAL = P * QT * (QT + 1) // 2

    ctx = ExitStack()
    with ctx:
        def sb(name, shape, dt, where=ctx):
            return where.enter_context(nc.sbuf_tensor(name, shape, dt))

        def pb(name, shape, dt):
            return ctx.enter_context(nc.psum_tensor(name, shape, dt))

        def sem(name):
            return ctx.enter_context(nc.semaphore(name))

        acc = sb("acc", [P, NT, D], F32)
        xt = sb("xt", [P, 2, KT, T], F16)
        wst = sb("wst", [P, 1280], F32)
        wst_q = wst[:, 0:512].rearrange("p (k c) -> p k c", k=KT)
        wst_o = wst[:, 512:1024]
        wst_k = wst[:, 1024:1152]
        wst_v = wst[:, 1152:1280]
        wring = sb("wring", [P, 12288], F16)
        wq = wring[:, 0:8192].rearrange("p (h s k c) -> p h s k c", h=2 * R, s=2, k=KT)
        wk = wring[:, 8192:10240].rearrange("p (h k s c) -> p h k s c", h=2, k=KT, s=2)
        wv = wring[:, 10240:12288].rearrange("p (h k s c) -> p h k s c", h=2, k=KT, s=2)
        ident = sb("ident", [P, P], F16)
        causal = sb("causal", [P, S], F32)
        slotu = sb("slotu", [P, TOP * NT], U32)
        yg = sb("yg", [P, 2, D], F32)
        wmax = sb("wmax", [P, 4, SCANS], F32)
        carrier = sb("carrier", [P, 2, 3], F32)
        wmax4 = sb("wmax4", [P, 4], F32)
        wall4 = sb("wall4", [P, 4], F32)
        wpow = sb("wpow", [P, 4], F32)
        winv = sb("winv", [P, 4], F32)
        wscale = sb("wscale", [P, 4], F32)
        score_scale = sb("score_scale", [P, 1], F32)
        neg_score_scale = sb("neg_score_scale", [P, 1], F32)
        out_scale = sb("out_scale", [P, 1], F32)
        tmp1 = sb("tmp1", [P, 2], F32)

        early = ExitStack()
        we = sb("we", [P, NE, 2, KT * D], F16, early)
        be = sb("be", [P, NE, D], F32, early)
        scan = sb("scan", [P, 2560], F32, early)
        xn = sb("xn", [P, 2, D], F32, early)
        xs = sb("xs", [P, 4, 2, D], F16, early)
        xg = wring[:, 0:3072].rearrange("p (r n) -> p r n", r=RING)
        y = wring[:, 4096:7168].bitcast(F32).rearrange("p (r d) -> p r d", r=RING)
        xgT = wring[:, 8192:11264].rearrange("p (r s k c) -> p r s k c", r=RING, s=2, k=KT)
        w32 = wring[:, :].bitcast(F32)
        be_flat = be[:, :, :].rearrange("p e n -> p (e n)")
        stage = [w32[:, 0:2048], w32[:, 2048:4096], w32[:, 4096:6144], scan[:, 0:2048],
                 be_flat[:, 0:2048], be_flat[:, 2048:4096], w32[:, 0:2048], w32[:, 2048:4096]]
        logits = wst[:, 0:128].rearrange("p (t e) -> p t e", t=NT)
        top8 = wst[:, 128:256].rearrange("p (t e) -> p t e", t=NT)
        top8i = wst[:, 256:384].bitcast(U32).rearrange("p (t e) -> p t e", t=NT)
        is1 = wst[:, 384:512].rearrange("p (t e) -> p t e", t=NT)
        is2 = wst[:, 512:640].rearrange("p (t e) -> p t e", t=NT)
        hot_row = wst[:, 640:896].bitcast(F16).rearrange("p (r c) -> p r c", r=4)
        past = wst[:, 896:896 + NS * NE].rearrange("p (n e) -> p n e", n=NS)
        bn = sb("bn", [P, QT, 6], F32, early)
        mv = sb("mv", [P, NT, 2], F32, early)
        std = sb("std", [P, NT], F32, early)
        rstd = sb("rstd", [P, NT], F32, early)
        nmr = sb("nmr", [P, NT], F32, early)
        eps = sb("eps", [P, 1], F32, early)
        wg32 = sb("wg32", [P, KT, NE], F32, early)
        wg = sb("wg", [P, 2, KT, NE], F16, early)
        bg = sb("bg", [P, NE], F32, early)
        iota8 = sb("iota8", [P, NE], F32, early)
        iotap = sb("iotap", [P, P], F16, early)
        iotas = sb("iotas", [P, NS], F32, early)
        iotan = sb("iotan", [P, NS], F32, early)
        token = sb("token", [P, NT], F32, early)
        before = sb("before", [P, P], F16, early)
        ones = sb("ones", [P, P], F16, early)
        top2 = sb("top2", [P, NT, TOP], F32, early)
        chosen = sb("chosen", [P, NT + 1, NE], F16, early)
        cnt = sb("cnt", [P, NE], I32, early)
        tiles_ = sb("tiles", [P, NE], I32, early)
        room = sb("room", [P, 2, 4 + NE], F32, early)
        size = sb("size", [P, NE], F32, early)
        base = sb("base", [P, NE], F32, early)
        slot_all = sb("slot_all", [P, NT, NE], F32, early)
        slotf = sb("slotf", [P, NT * TOP], F32, early)
        sloti = sb("sloti", [P, NT * TOP], I32, early)
        rowi = sb("rowi", [P, NT * TOP], I32, early)
        tilei = sb("tilei", [P, NT * TOP], I32, early)
        rowf = sb("rowf", [P, NT * TOP], F32, early)
        tilef = sb("tilef", [P, NT * TOP], F32, early)
        hot_tile = sb("hot_tile", [P, 4, NS], F16, early)
        expf = sb("expf", [P, NS], F32, early)
        expi = sb("expi", [P, NS], I32, early)
        source = sb("source", [P, NS], U32, early)
        emax = sb("emax", [P, NE + 1], F32, early)
        eall = sb("eall", [P, NE + 1], F32, early)
        epow = sb("epow", [P, NE + 1], F32, early)
        einv = sb("einv", [P, NE + 1], F32, early)
        escale = sb("escale", [P, NE + 1], F32, early)
        eundo = sb("eundo", [P, NE + 1], F32, early)
        early.close()

        wo = sb("wo", [P, 2 * R, 2, D], F16)
        stage_w = sb("stage_w", [P, 3 * 512], F32)
        kT = sb("kT", [P, 2, S], F16)
        vT = sb("vT", [P, 2, S], F16)
        vs = sb("vs", [P, 2, QT, HEAD], F16)
        qT = sb("qT", [P, 2, 2, S], F16)
        pr = sb("pr", [P, 2, CAUSAL], F32)
        ps_split = sb("ps_split", [P, 2, 2, CAUSAL], F16)
        pT = sb("pT", [P, 2, 2, CAUSAL], F16)
        oT = sb("oT", [P, 2, R, 2, S], F16)
        rowmax = sb("rowmax", [P, 2, QT], F32)
        negmax = sb("negmax", [P, 2, QT], F32)
        rowsum = sb("rowsum", [P, 2, QT], F32)
        rinv = sb("rinv", [P, 2, QT], F32)

        gen = [pb(f"gen{i}", [P, 512], F32) for i in range(3)]
        sco = [pb(f"sco{i}", [P, 512], F32) for i in range(3)]
        att = [pb(f"att{i}", [P, 512], F32) for i in range(2)]
        tra = [sco[i][:, :].bitcast(F16) for i in range(2)]
        ybank = sco
        xbank = [bank[:, :].bitcast(F16) for bank in (gen[2], att[0], att[1])]

        x_loaded = [sem(f"x_loaded{b}") for b in range(B)]
        gate_loaded = sem("gate_loaded")
        we_loaded = [sem(f"we_loaded{e}") for e in range(NE)]
        be_loaded = sem("be_loaded")
        scan_loaded = sem("scan_loaded")
        first_loaded = sem("first_loaded")
        w_loaded = sem("w_loaded")
        next_loaded = sem("next_loaded")
        stored = sem("stored")
        consts = sem("consts")
        dve_chain = sem("dve_chain")
        stats_done = sem("stats_done")
        std_done = sem("std_done")
        rstd_done = sem("rstd_done")
        xn_done = sem("xn_done")
        xhi_done = sem("xhi_done")
        xlo_done = sem("xlo_done")
        xrow_stored = [sem(f"xrow_stored{i}") for i in range(4)]
        xt_filled = sem("xt_filled")
        xt_done = sem("xt_done")
        emax_done = sem("emax_done")
        eall_done = sem("eall_done")
        escale_done = sem("escale_done")
        wghi_done = sem("wghi_done")
        wg_done = sem("wg_done")
        we_hi = sem("we_hi")
        we_scaled = sem("we_scaled")
        we_done = sem("we_done")
        gate_filled = sem("gate_filled")
        chosen_done = sem("chosen_done")
        rank_filled = sem("rank_filled")
        hot_done = sem("hot_done")
        hot_used = sem("hot_used")
        routed = sem("routed")
        xg_loaded = [sem(f"xg_loaded{i}") for i in range(RING)]
        xg_filled = sem("xg_filled")
        xgT_free = sem("xgT_free")
        y_filled = sem("y_filled")
        ybank_free = sem("ybank_free")
        relu_done = sem("relu_done")
        y_free = [sem(f"y_free{i}") for i in range(RING)]
        yg_loaded = sem("yg_loaded")
        ffn_added = sem("ffn_added")
        scan_free = sem("scan_free")
        wmax_done = sem("wmax_done")
        wall_done = sem("wall_done")
        wscale_done = sem("wscale_done")
        first_hi = sem("first_hi")
        first_ready = sem("first_ready")
        w_hi = sem("w_hi")
        w_ready = sem("w_ready")
        q_filled, q_hi, q_ready = sem("q_filled"), sem("q_hi"), sem("q_ready")
        k_filled, k_hi, k_ready = sem("k_filled"), sem("k_hi"), sem("k_ready")
        v_filled, v_hi, v_ready = sem("v_filled"), sem("v_hi"), sem("v_ready")
        s_filled = sem("s_filled")
        s_masked = sem("s_masked")
        bias_ready = sem("bias_ready")
        exp_done = sem("exp_done")
        rinv_done = sem("rinv_done")
        p_hi = sem("p_hi")
        p_split = sem("p_split")
        pt_ready = [sem(f"pt_ready{i}") for i in range(2)]
        vs_ready = sem("vs_ready")
        sp_steps = sem("sp_steps")
        o_filled, o_hi, o_ready = sem("o_filled"), sem("o_hi"), sem("o_ready")
        out_filled, out_added = sem("out_filled"), sem("out_added")

        x_v = x.rearrange("b (t p) d -> b p t d", p=P)
        out_v = out.rearrange("b (t p) d -> b p t d", p=P)
        wq_v = w_q.rearrange("(k p) c -> p k c", p=P)
        wk_v = w_k.rearrange("(k p) c -> p k c", p=P)
        wv_v = w_v.rearrange("(k p) c -> p k c", p=P)
        wo_v = w_o.rearrange("(h p) n -> p h n", p=P)
        xrows = nc.dram_tensor("xrows", [T, 2 * D], F16, kind="Internal").ap()
        yrows = nc.dram_tensor("yrows", [NS * P, D], F32, kind="Internal").ap()
        scan_v = [(w.rearrange("(p a) n -> p (a n)", p=P), w.shape[0] * w.shape[1] // P // SCANS)
                  for w in (w_q, w_k, w_v, w_o)]
        SCAN_AT = [sum(n for _, n in scan_v[:i]) for i in range(4)]

        def scanned(i):
            return scan[:, SCAN_AT[i]:SCAN_AT[i] + scan_v[i][1]]

        FIRST = [(scan[:, 512 * i:512 * (i + 1)].rearrange("p (k c) -> p k c", k=KT), view[:, :, h * HEAD:(h + 1) * HEAD],
                  dst, m)
                 for i, (view, h, dst, m) in enumerate(((wk_v, 0, lambda s: wk[:, 0, :, s, :], 1),
                                                        (wq_v, 0, lambda s: wq[:, 0, s], 0),
                                                        (wq_v, 1, lambda s: wq[:, 1, s], 0),
                                                        (wq_v, 2, lambda s: wq[:, 2, s], 0),
                                                        (wv_v, 0, lambda s: wv[:, 0, :, s, :], 2)))]

        NEXT = [(stage_w[:, 0:512].rearrange("p (k c) -> p k c", k=KT), wq_v[:, :, 4 * HEAD:5 * HEAD],
                 lambda s: wq[:, 4, s], 0)]
        NEXT += [(stage_w[:, 512 * i:512 * (i + 1)], wo_v[:, i, :], lambda s, i=i: wo[:, i, s, :], 3) for i in (1, 2)]

        block = ctx.enter_context(nc.Block())

        @block.sync
        def _(sp):
            for b in range(B):
                sp.dma_start(acc[:, b * QT:(b + 1) * QT, :], x_v[b]).then_inc(x_loaded[b], 16)
            sp.dma_start(wg32[:, :, :], w_gate.rearrange("(k p) e -> p k e", p=P)).then_inc(gate_loaded, 16)
            sp.dma_start(bg[:, :], b_gate.partition_broadcast(P)).then_inc(gate_loaded, 16)

            def load_expert(e):
                sp.dma_start(stage[e].rearrange("p (k n) -> p k n", k=KT),
                             w_e[e].rearrange("(k p) n -> p k n", p=P)).then_inc(we_loaded[e], 16)

            for e in range(6):
                load_expert(e)
            for t in range(NT):
                sp.wait_ge(xlo_done, t + 1)
                sp.dma_start(xrows[t * P:(t + 1) * P, :],
                             xs[:, t % 4].rearrange("p s d -> p (s d)")).then_inc(xrow_stored[t % 4], 16)
                if t in (10, 12):
                    e = 6 + (t - 10) // 2
                    sp.wait_ge(we_done, e - 5)
                    load_expert(e)
            sp.wait_ge(we_done, 6)
            sp.dma_start(be[:, :, :], b_e.partition_broadcast(P)).then_inc(be_loaded, 16)

            def load_scan(c):
                sp.wait_ge(scan_free, c + 1)
                for i, (view, n) in enumerate(scan_v):
                    sp.dma_start(scanned(i), view[:, bass.ds(c * n, n)]).then_inc(scan_loaded, 16)

            def store_y(u, k):
                sp.wait_ge(relu_done, RING * u + k + 1)
                sp.dma_start(yrows[bass.ds((RING * u + k) * P, P), :], y[:, k, :]).then_inc(y_free[k], 16)

            for c in range(EARLY_SCANS):
                load_scan(c)
            with sp.Fori(0, NS // RING - 1) as u:
                load_scan(u + EARLY_SCANS)
                for k in range(RING):
                    store_y(u, k)
            sp.wait_ge(scan_free, SCANS + 1)
            for where, src, _, _ in FIRST:
                sp.dma_start(where, src).then_inc(first_loaded, 16)

            def load_piece(q, kv, o):
                sp.dma_start(wst_q, wq_v[:, :, bass.ds(q * HEAD, HEAD)]).then_inc(w_loaded, 16)
                block, col = bass.ds(kv % KT, 1), bass.ds((kv // R) * HEAD, HEAD)
                sp.dma_start(wst_k, wk_v[:, block, col]).then_inc(w_loaded, 16)
                sp.dma_start(wst_v, wv_v[:, block, col]).then_inc(w_loaded, 16)
                sp.dma_start(wst_o, wo_v[:, bass.ds(o, 1), :]).then_inc(w_loaded, 16)

            load_piece(3, 4, 0)
            for k in range(RING):
                store_y(NS // RING - 1, k)
            sp.wait_ge(ybank_free, NS + RING)
            for where, src, _, _ in NEXT:
                sp.dma_start(where, src).then_inc(next_loaded, 16)

            def transpose_p(h, slot):
                sp.wait_ge(p_split, h + 1)
                sp.sem_inc(sp_steps, 1)
                if not (isinstance(h, int) and h < 2):
                    sp.wait_ge(o_filled, h - 1)
                    sp.sem_inc(sp_steps, 1)
                sp.dma_start(pT[:, slot].rearrange("p s (b c) -> p (s b) c", c=P),
                             ps_split[:, slot].rearrange("p s c -> p (s c)"), transpose=True).then_inc(pt_ready[slot], 16)

            def transpose_v(it):
                sp.wait_ge(v_ready, it + 1)
                sp.sem_inc(sp_steps, 1)
                if not (isinstance(it, int) and it == 0):
                    sp.wait_ge(o_filled, R * it)
                    sp.sem_inc(sp_steps, 1)
                sp.dma_start(vs[:, :, :, :].rearrange("p s t d -> p (s t) d"),
                             vT[:, :, :].rearrange("p s c -> p (s c)"), transpose=True).then_inc(vs_ready, 16)

            def pair(it, last=False):
                for r in range(R):
                    if not (last and r == R - 1):
                        transpose_p(it * R + r + 1, (r + 1) % 2)
                    if r == 0:
                        transpose_v(it)
                    if r == 0 and not last:
                        sp.wait_ge(w_ready, it + 1)
                        load_piece((it + 5) % NQ, (it + 5) % NQ, (it + 3) % NQ)

            transpose_p(0, 0)
            pair(0)
            with sp.Fori(1, NIT - 1) as it:
                pair(it)
            pair(NIT - 1, last=True)
            for b in range(B - 1):
                sp.wait_ge(out_added, QT * (NIT - B + b + 1))
                sp.dma_start(out_v[b], acc[:, b * QT:(b + 1) * QT, :]).then_inc(stored, 16)
            for t in range(QT):
                sp.wait_ge(out_added, QT * (NIT - 1) + t + 1)
                sp.dma_start(out_v[B - 1][:, t, :], acc[:, (B - 1) * QT + t, :]).then_inc(stored, 16)
            sp.wait_ge(stored, 16 * (B - 1 + QT))

        @block.gpsimd
        def _(pool):
            pool.memset(ident[:, :], 0.0).then_inc(consts, 1)
            pool.memset(causal[:, :], 0.0).then_inc(consts, 1)
            pool.wait_ge(consts, 2)
            pool.affine_select(out=ident[:, :], in_=ident[:, :], compare_op=ALU.not_equal, fill=1.0, base=0,
                               pattern=[[-1, P]], channel_multiplier=1).then_inc(consts, 1)
            pool.affine_select(out=causal[:, S - P:S], in_=causal[:, S - P:S], compare_op=ALU.is_ge, fill=MASKED,
                               base=0, pattern=[[-1, P]], channel_multiplier=1).then_inc(consts, 1)
            pool.iota(iota8[:, :], pattern=[[1, NE]], base=0, channel_multiplier=0,
                      allow_small_or_imprecise_dtypes=True).then_inc(consts, 1)
            pool.iota(iotap[:, :], pattern=[[1, P]], base=0, channel_multiplier=0,
                      allow_small_or_imprecise_dtypes=True).then_inc(consts, 1)
            pool.iota(iotas[:, :], pattern=[[P, NS]], base=0, channel_multiplier=0,
                      allow_small_or_imprecise_dtypes=True).then_inc(consts, 1)
            pool.iota(iotan[:, :], pattern=[[1, NS]], base=0, channel_multiplier=0,
                      allow_small_or_imprecise_dtypes=True).then_inc(consts, 1)
            pool.iota(token[:, :], pattern=[[P, NT]], base=0, channel_multiplier=1,
                      allow_small_or_imprecise_dtypes=True).then_inc(consts, 1)
            pool.memset(ones[:, :], 1.0).then_inc(consts, 1)
            pool.memset(before[:, :], 0.0).then_inc(consts, 1)
            pool.wait_ge(consts, 11)
            pool.affine_select(out=before[:, :], in_=before[:, :], compare_op=ALU.is_ge, fill=1.0, base=0,
                               pattern=[[-1, P]], channel_multiplier=1).then_inc(consts, 1)

            def all_max(i):
                cols = slice(2 * i + (i > 0), 2 * i + 3)
                pool.wait_ge(emax_done, i + 1)
                pool.partition_all_reduce(eall[:, cols], emax[:, cols], P, ABSMAX).then_inc(eall_done, 1)

            def expert_lo(e):
                pool.wait_ge(we_scaled, e + 1)
                pool.tensor_tensor(we[:, e, LO, :], stage[e], we[:, e, HI, :], ALU.subtract).then_inc(we_done, 1)

            all_max(0)
            all_max(1)
            expert_lo(0)
            expert_lo(1)
            all_max(2)
            for e in range(2, 6):
                expert_lo(e)
            all_max(3)
            expert_lo(6)
            expert_lo(7)
            pool.wait_ge(routed, 1)
            pool.wait_ge(we_done, NE)
            for i in range(4):
                pool.wait_ge(xrow_stored[i], 16 * NT // 4)
            for i in range(NS):
                if i >= RING:
                    pool.wait_ge(xg_filled, i - RING + 1)
                pool.indirect_dma_start(out=xg[:, i % RING, :], out_offset=None, in_=xrows,
                                        in_offset=bass.IndirectOffsetOnAxis(ap=source[:, i:i + 1], axis=0)
                                        ).then_inc(xg_loaded[i % RING], 16)
            pool.wait_ge(wmax_done, 1)
            pool.partition_all_reduce(wall4[:, :], wmax4[:, :], P, ABSMAX).then_inc(wall_done, 1)
            for k in range(RING):
                pool.wait_ge(y_free[k], 16 * (NS // RING + 1))
            for j in range(TOP * NT):
                if j:
                    pool.wait_ge(yg_loaded, 16 * j)
                if j >= 2:
                    pool.wait_ge(ffn_added, j - 1)
                pool.indirect_dma_start(out=yg[:, j % 2, :], out_offset=None, in_=yrows,
                                        in_offset=bass.IndirectOffsetOnAxis(ap=slotu[:, j:j + 1], axis=0)
                                        ).then_inc(yg_loaded, 16)

        @block.scalar
        def _(act):
            act.wait_ge(stats_done, 1)

            def deviations(b):
                act.wait_ge(stats_done, b + 2)
                act.activation(std[:, b * QT:(b + 1) * QT], mv[:, b * QT:(b + 1) * QT, 1], ACT.Sqrt,
                               bias=eps[:, 0:1]).then_inc(std_done, 1)

            def normalise(t):
                if t % QT == 0:
                    act.wait_ge(rstd_done, t // QT + 1)
                if t >= 2:
                    act.wait_ge(xlo_done, t - 1)
                act.activation(xn[:, t % 2, :], acc[:, t, :], ACT.Identity, bias=nmr[:, t:t + 1],
                               scale=rstd[:, t:t + 1]).then_inc(xn_done, 1)
                if t >= 4:
                    act.wait_ge(xt_filled, t - 3)
                    act.wait_ge(xrow_stored[t % 4], 16 * (t // 4))
                act.wait_ge(xn_done, t + 1)
                act.activation(xs[:, t % 4, HI, :], xn[:, t % 2, :], ACT.Copy).then_inc(xhi_done, 1)

            def copy_xt(t):
                act.wait_ge(xt_filled, t + 1)
                act.activation(xt[:, :, :, t * P:(t + 1) * P],
                               tra[t % 2][:, :].rearrange("p (s k c) -> p s k c", s=2, k=KT),
                               ACT.Copy).then_inc(xt_done, 1)

            def expert_hi(e):
                act.wait_ge(escale_done, e // 2 + 1)
                scale = escale[:, e + 1:e + 2]
                act.activation(we[:, e, HI, :], stage[e], ACT.Copy, scale=scale).then_inc(we_hi, 1)
                act.wait_ge(we_hi, e + 1)
                act.activation(stage[e], stage[e], ACT.Copy, scale=scale).then_inc(we_scaled, 1)

            deviations(0)
            for t in range(NT):
                normalise(t)
                if t:
                    copy_xt(t - 1)
                if t % QT == 1 and t + QT < NT:
                    deviations(t // QT + 1)
                if t == 7:
                    act.wait_ge(escale_done, 1)
                    act.activation(wg[:, HI], wg32[:, :, :], ACT.Copy, scale=escale[:, 0:1]).then_inc(wghi_done, 1)
                    expert_hi(0)
                    expert_hi(1)
            copy_xt(NT - 1)
            for e in range(2, NE):
                expert_hi(e)

            def copy_xg(u, k):
                i = RING * u + k
                act.wait_ge(xg_filled, i + 1)
                act.activation(xgT[:, k], xbank[k].rearrange("p (s k c) -> p s k c", s=2, k=KT),
                               ACT.Copy).then_inc(xgT_free, 1)

            def relu(u, k):
                act.wait_ge(ybank_free, RING * u + k + 1 + RING)
                act.activation(y[:, k, :], y[:, k, :], ACT.Relu, scale=0.5).then_inc(relu_done, 1)

            act.wait_ge(we_done, NE)
            copy_xg(0, 0)
            with act.Fori(0, NS // RING - 1) as u:
                for k in range(RING):
                    copy_xg(u + (k + 1) // RING, (k + 1) % RING)
                    relu(u, k)
            for k in range(RING):
                if k + 1 < RING:
                    copy_xg(NS // RING - 1, k + 1)
                relu(NS // RING - 1, k)

            act.wait_ge(wscale_done, 1)

            def first_high(i):
                where, _, dst, m = (FIRST + NEXT)[i]
                act.activation(dst(HI), where, ACT.Copy, scale=wscale[:, m:m + 1]).then_inc(first_hi, 1)

            def weights_hi(piece, q, kv, o):
                act.wait_ge(w_loaded, 64 * (piece + 1))
                act.activation(wq[:, bass.ds(q % (2 * R), 1), HI], wst_q, ACT.Copy, scale=wscale[:, 0:1])
                group, block = bass.ds((kv // R) % 2, 1), bass.ds(kv % KT, 1)
                act.activation(wk[:, group, block, HI], wst_k, ACT.Copy, scale=wscale[:, 1:2])
                act.activation(wv[:, group, block, HI], wst_v, ACT.Copy, scale=wscale[:, 2:3])
                act.activation(wo[:, bass.ds(o % (2 * R), 1), HI], wst_o, ACT.Copy,
                               scale=wscale[:, 3:4]).then_inc(w_hi, 1)

            def q_high(bank, h, slot):
                act.wait_ge(q_filled, h + 1)
                act.activation(qT[:, slot, HI, :], gen[bank][:, :], ACT.Copy).then_inc(q_hi, 1)

            def k_high(bank, it):
                act.wait_ge(k_filled, it + 1)
                act.activation(kT[:, HI, :], gen[bank][:, :], ACT.Copy).then_inc(k_hi, 1)

            def v_high(bank, it):
                if not (isinstance(it, int) and it == 0):
                    act.wait_ge(vs_ready, 16 * it)
                act.wait_ge(v_filled, it + 1)
                act.activation(vT[:, HI, :], gen[bank][:, :], ACT.Copy).then_inc(v_hi, 1)

            def exps(h, slot):
                act.wait_ge(bias_ready, h + 1)
                for i in range(QT):
                    a = SCORE_AT[i]
                    row = pr[:, slot, a:a + P * (i + 1)]
                    last = act.activation(row, row, ACT.Exp, bias=negmax[:, slot, i:i + 1],
                                          scale=score_scale[:, 0:1], accum_out=rowsum[:, slot, i:i + 1])
                last.then_inc(exp_done, 1)

            def o_high(h, it, r):
                act.wait_ge(o_filled, h + 1)
                act.activation(oT[:, bass.ds(it % 2, 1), r, HI, :], att[r % 2][:, :], ACT.Copy).then_inc(o_hi, 1)

            act.wait_ge(first_loaded, 16 * len(FIRST))
            for i in range(len(FIRST)):
                first_high(i)
            for k in range(RING):
                act.wait_ge(y_free[k], 16 * (NS // RING + 1))
            weights_hi(0, 3, 4, 0)
            k_high(0, 0)
            q_high(1, 0, 0)
            q_high(2, 1, 1)
            act.wait_ge(next_loaded, 16 * len(NEXT))
            for i in range(len(NEXT)):
                first_high(len(FIRST) + i)
            exps(0, 0)
            q_high(0, 2, 0)
            exps(1, 1)

            def pair(it, first=False, last=False):
                for r in range(R):
                    n = it * R + r
                    if r != 3 and not (last and r >= 1):
                        q_high(Q_BANK[r], n + 3, (r + 1) % 2)
                    if r == 1 and not last:
                        k_high(K_BANK, it + 1)
                    if r == 3 and not last:
                        q_high(Q_BANK[r], n + 3, (r + 1) % 2)
                    if r == 0:
                        v_high(V_BANK, it)
                    if not (first and r == 0):
                        o_high(n - 1, it if r else it - 1, (r - 1) % R)
                    if not (last and r >= 2):
                        exps(n + 2, r % 2)
                    if r == 2 and not last:
                        act.wait_ge(k_filled, it + 2)
                        weights_hi(it + 1, it + 5, it + 5, it + 3)

            pair(0, first=True)
            with act.Fori(1, NIT - 1) as it:
                pair(it)
            pair(NIT - 1, last=True)
            o_high(NH - 1, NIT - 1, R - 1)

        @block.vector
        def _(dve):
            chain = [0]

            def link(ins):
                chain[0] += 1
                ins.then_inc(dve_chain, 1)
                dve.wait_ge(dve_chain, chain[0])

            def powers(allmax, pow2, inv, scale):
                link(dve.tensor_scalar(pow2, allmax, 2.0 ** -60, None, ALU.max))
                link(dve.tensor_scalar(pow2.bitcast(I32), pow2.bitcast(I32), 0x7F800000, None, ALU.bitwise_and))
                link(dve.reciprocal(inv, pow2))
                return dve.tensor_scalar(scale, inv, 8.0, None, ALU.mult)

            dve.memset(eps[:, :], EPS).then_inc(stats_done, 1)
            dve.memset(room[:, :, :], 0.0)
            dve.memset(chosen[:, NT, :], 0.0)
            for k in range(RING):
                dve.memset(tmp1[:, 0:1] if k == 0 else tmp1[:, 1:2] if k == 1 else carrier[:, 0, 0:1], 0.0
                           ).then_inc(y_free[k], 16)
            dve.memset(carrier[:, 0, 1:2], 0.0).then_inc(scan_free, 1)
            dve.memset(carrier[:, 0, 2:3], 0.0).then_inc(xgT_free, RING)
            link(dve.memset(carrier[:, 1, 0:1], 0.0))

            def stats(b):
                tiles = range(b * QT, (b + 1) * QT)
                dve.wait_ge(x_loaded[b], 16)
                for t in tiles:
                    ins = dve.bn_stats(bn[:, t % QT, :], acc[:, t, :])
                link(ins)
                for t in tiles:
                    ins = dve.bn_aggr(mv[:, t, :], bn[:, t % QT, :])
                ins.then_inc(stats_done, 1)

            def inverse(b):
                cols = slice(b * QT, (b + 1) * QT)
                dve.wait_ge(std_done, b + 1)
                link(dve.reciprocal(rstd[:, cols], std[:, cols]))
                dve.scalar_tensor_tensor(out=nmr[:, cols], in0=mv[:, cols, 0], scalar=-1.0, in1=rstd[:, cols],
                                         op0=ALU.mult, op1=ALU.mult).then_inc(rstd_done, 1)

            def low(t):
                dve.wait_ge(xhi_done, t + 1)
                dve.tensor_tensor(xs[:, t % 4, LO, :], xn[:, t % 2, :], xs[:, t % 4, HI, :],
                                  ALU.subtract).then_inc(xlo_done, 1)

            def expert_max(e):
                dve.wait_ge(we_loaded[e], 16)
                ins = dve.tensor_reduce(emax[:, e + 1:e + 2], stage[e], AX_X, ALU.max, apply_absolute_value=True)
                if e % 2:
                    ins.then_inc(emax_done, 1)

            def expert_scales(i):
                cols = slice(2 * i + (i > 0), 2 * i + 3)
                dve.wait_ge(eall_done, i + 1)
                link(powers(eall[:, cols], epow[:, cols], einv[:, cols], escale[:, cols]))
                dve.tensor_scalar(eundo[:, cols], epow[:, cols], 0.125, None, ALU.mult).then_inc(escale_done, 1)

            stats(0)
            inverse(0)
            for t in range(NT):
                low(t)
                if t % QT == 1 and t + QT < NT:
                    stats(t // QT + 1)
                if t % QT == 2 and t + QT < NT:
                    inverse(t // QT + 1)
                if t == 3:
                    dve.wait_ge(gate_loaded, 32)
                    dve.tensor_reduce(emax[:, 0:1], wg32[:, :, :], mybir.AxisListType.XY, ALU.max,
                                      apply_absolute_value=True)
                if t in (3, 4, 6, 7, 8, 9, 13, 14):
                    expert_max((3, 4, 6, 7, 8, 9, 13, 14).index(t))
                if t in (6, 9, 11):
                    expert_scales((6, 9, 11).index(t))
                if t == 7:
                    dve.wait_ge(wghi_done, 1)
                    dve.scalar_tensor_tensor(out=wg[:, LO], in0=wg32[:, :, :], scalar=escale[:, 0:1], in1=wg[:, HI],
                                             op0=ALU.mult, op1=ALU.subtract).then_inc(wg_done, 1)

            dve.wait_ge(gate_filled, 1)
            link(dve.scalar_tensor_tensor(out=logits[:, :, :],
                                          in0=gen[0][:, 0:NT * NE].rearrange("p (t e) -> p t e", t=NT),
                                          scalar=eundo[:, 0:1], in1=bg[:, :].unsqueeze(1).broadcast_to([P, NT, NE]),
                                          op0=ALU.mult, op1=ALU.add))
            for t in range(NT):
                ins = dve.max(top8[:, t, :], logits[:, t, :])
            link(ins)
            for t in range(NT):
                ins = dve.max_index(top8i[:, t, :], top8[:, t, :], logits[:, t, :])
            link(ins)
            link(dve.tensor_copy(top2[:, :, :], top8i[:, :, 0:TOP]))
            dve.wait_ge(consts, 12)
            all_iota = iota8[:, :].unsqueeze(1).broadcast_to([P, NT, NE])
            dve.tensor_tensor(is1[:, :, :], all_iota, top2[:, :, 0:1].broadcast_to([P, NT, NE]), ALU.is_equal)
            link(dve.tensor_tensor(is2[:, :, :], all_iota, top2[:, :, 1:2].broadcast_to([P, NT, NE]), ALU.is_equal))
            dve.tensor_tensor(chosen[:, 0:NT, :], is1[:, :, :], is2[:, :, :], ALU.add).then_inc(chosen_done, 1)
            expert_scales(3)

            dve.wait_ge(rank_filled, 1)
            ranks = gen[1][:, 0:NT * NE].rearrange("p (t e) -> p t e", t=NT)
            link(dve.tensor_scalar(cnt[:, :], gen[1][:, NT * NE:(NT + 1) * NE], float(P - 1), None, ALU.add))
            link(dve.tensor_scalar(tiles_[:, :], cnt[:, :], 7, None, ALU.arith_shift_right))
            dve.tensor_scalar(size[:, :], tiles_[:, :], float(P), None, ALU.mult)
            link(dve.tensor_scalar(room[:, 0, 4:4 + NE], tiles_[:, :], float(P), None, ALU.mult))
            for i, d in enumerate((1, 2, 4)):
                link(dve.tensor_tensor(room[:, (i + 1) % 2, 4:4 + NE], room[:, i % 2, 4:4 + NE],
                                       room[:, i % 2, 4 - d:4 + NE - d], ALU.add))
            until = room[:, 1, 4:4 + NE]
            link(dve.tensor_tensor(base[:, :], until, size[:, :], ALU.subtract))
            link(dve.tensor_tensor(slot_all[:, :, :], ranks, base[:, :].unsqueeze(1).broadcast_to([P, NT, NE]), ALU.add))
            dve.tensor_tensor(is1[:, :, :], is1[:, :, :], slot_all[:, :, :], ALU.mult)
            link(dve.tensor_tensor(is2[:, :, :], is2[:, :, :], slot_all[:, :, :], ALU.mult))
            slot2 = slotf[:, :].rearrange("p (t k) -> p t k", k=TOP)
            dve.tensor_reduce(slot2[:, :, 0], is1[:, :, :], AX_X, ALU.add)
            link(dve.tensor_reduce(slot2[:, :, 1], is2[:, :, :], AX_X, ALU.add))
            dve.tensor_copy(slotu[:, :], slotf[:, :])
            link(dve.tensor_copy(sloti[:, :], slotf[:, :]))
            dve.tensor_scalar(rowi[:, :], sloti[:, :], P - 1, None, ALU.bitwise_and)
            link(dve.tensor_scalar(tilei[:, :], sloti[:, :], 7, None, ALU.arith_shift_right))
            dve.tensor_copy(rowf[:, :], rowi[:, :])
            link(dve.tensor_copy(tilef[:, :], tilei[:, :]))
            for j in range(TOP * NT):
                if j >= 4:
                    dve.wait_ge(hot_used, j - 3)
                dve.tensor_scalar(hot_row[:, j % 4, :], iotap[:, :], rowf[:, j:j + 1], None, ALU.is_equal)
                dve.tensor_scalar(hot_tile[:, j % 4, :], iotan[:, :], tilef[:, j:j + 1], token[:, j // TOP:j // TOP + 1],
                                  ALU.is_equal, ALU.mult).then_inc(hot_done, 1)
            link(dve.tensor_tensor(past[:, :, :], iotas[:, :].unsqueeze(2).broadcast_to([P, NS, NE]),
                                   until.unsqueeze(1).broadcast_to([P, NS, NE]), ALU.is_ge))
            link(dve.tensor_reduce(expf[:, :], past[:, :, :], AX_X, ALU.add))
            link(dve.tensor_scalar(expi[:, :], expf[:, :], float(NE - 1), None, ALU.min))
            dve.wait_ge(hot_used, TOP * NT)
            dve.tensor_copy(source[:, :], gen[0][:, 0:NS]).then_inc(routed, 1)
            dve.memset(carrier[:, 1, 1:2], 0.0).then_inc(ybank_free, RING)

            def scan_max(c):
                dve.wait_ge(scan_loaded, 64 * (c + 1))
                for i in range(4):
                    ins = dve.tensor_reduce(wmax[:, i, bass.ds(c, 1)], scanned(i), AX_X, ALU.max,
                                            apply_absolute_value=True)
                ins.then_inc(scan_free, 1)

            def expert_out(u, k):
                i = RING * u + k
                e = dve.value_load(expi[0:1, bass.ds(i, 1)], min_val=0, max_val=NE - 1)
                dve.wait_ge(y_free[k], 16 * (u + 1))
                dve.wait_ge(y_filled, i + 1)
                dve.scalar_tensor_tensor(out=y[:, k, :], in0=ybank[k][:, :], scalar=eundo[:, bass.ds(e + 1, 1)],
                                         in1=be[:, bass.ds(e, 1), :].rearrange("p e n -> p (e n)"),
                                         op0=ALU.mult, op1=ALU.add).then_inc(ybank_free, 1)

            for c in range(EARLY_SCANS):
                scan_max(c)
            dve.wait_ge(routed, 1)
            dve.wait_ge(escale_done, 4)
            dve.wait_ge(be_loaded, 16)
            dve.wait_ge(we_done, NE)
            with dve.Fori(0, NS // RING - 1) as u:
                for k in range(RING):
                    expert_out(u, k)
                scan_max(u + EARLY_SCANS)

            dve.wait_ge(scan_free, SCANS + 1)
            dve.tensor_reduce(wmax4[:, :], wmax[:, :, :], AX_X, ALU.max).then_inc(wmax_done, 1)
            for k in range(RING):
                expert_out(NS // RING - 1, k)
            dve.wait_ge(wall_done, 1)
            link(powers(wall4[:, :], wpow[:, :], winv[:, :], wscale[:, :]))
            link(dve.tensor_scalar(tmp1[:, 0:1], wpow[:, 0:1], wpow[:, 1:2], HEAD ** -0.5 / 64, ALU.mult, ALU.mult))
            dve.tensor_copy(score_scale[:, :], tmp1[:, 0:1])
            dve.tensor_scalar(neg_score_scale[:, :], tmp1[:, 0:1], -1.0, None, ALU.mult)
            link(dve.tensor_scalar(out_scale[:, :], wpow[:, 2:3], wpow[:, 3:4], 1.0 / 64, ALU.mult, ALU.mult))
            dve.tensor_copy(tmp1[:, 0:1], out_scale[:, :]).then_inc(wscale_done, 1)

            def lower(dst, src, high, m):
                return dve.scalar_tensor_tensor(out=dst, in0=src, scalar=wscale[:, m:m + 1], in1=high,
                                                op0=ALU.mult, op1=ALU.subtract)

            def first_low(i):
                where, _, dst, m = (FIRST + NEXT)[i]
                dve.wait_ge(first_hi, i + 1)
                lower(dst(LO), where, dst(HI), m).then_inc(first_ready, 1)

            def weights_lo(piece, q, kv, o):
                dve.wait_ge(w_hi, piece + 1)
                a = wq[:, bass.ds(q % (2 * R), 1)]
                lower(a[:, :, LO].rearrange("p e k c -> p (e k c)"), wst[:, 0:512],
                      a[:, :, HI].rearrange("p e k c -> p (e k c)"), 0)
                for w, src, m in ((wk, wst_k, 1), (wv, wst_v, 2)):
                    a = w[:, bass.ds((kv // R) % 2, 1), bass.ds(kv % KT, 1)]
                    lower(a[:, :, :, LO].rearrange("p a b c -> p (a b c)"), src,
                          a[:, :, :, HI].rearrange("p a b c -> p (a b c)"), m)
                a = wo[:, bass.ds(o % (2 * R), 1)]
                lower(a[:, :, LO].rearrange("p e n -> p (e n)"), wst_o,
                      a[:, :, HI].rearrange("p e n -> p (e n)"), 3).then_inc(w_ready, 1)

            def add_ffn(it, first):
                if not first:
                    dve.wait_ge(out_added, QT * (it - 1) + 2)
                dve.wait_ge(yg_loaded, 16 * it + 16)
                a = acc[:, bass.ds(it // TOP, 1), :]
                dve.tensor_tensor(a, a, yg[:, bass.ds(it % TOP, 1), :], ALU.add).then_inc(ffn_added, 1)

            def mask_rows(h, slot, fills=(0, 1, 2)):
                if not (isinstance(h, int) and h < 2) and 0 in fills:
                    dve.wait_ge(p_split, h - 1)
                for u in fills:
                    tiles = SCORE_FILLS[u]
                    dve.wait_ge(s_filled, 3 * h + u + 1)
                    dve.memset(carrier[:, slot, u:u + 1], 0.0)
                    at = 0
                    for i in tiles:
                        w = P * (i + 1)
                        a = SCORE_AT[i]
                        ins = dve.tensor_tensor_reduce(pr[:, slot, a:a + w], sco[u][:, at:at + w],
                                                       causal[:, S - w:S], 1.0, LOWEST, ALU.add, ALU.max,
                                                       rowmax[:, slot, i:i + 1])
                        at += w
                    ins.then_inc(s_masked, 1)
                if 2 not in fills:
                    return
                dve.wait_ge(s_masked, 3 * h + 3)
                dve.tensor_scalar(negmax[:, slot, :], rowmax[:, slot, :], neg_score_scale[:, 0:1], None,
                                  ALU.mult).then_inc(bias_ready, 1)

            def split_hi(h, slot):
                dve.wait_ge(exp_done, h + 1)
                dve.reciprocal(rinv[:, slot, :], rowsum[:, slot, :]).then_inc(rinv_done, 1)
                if not (isinstance(h, int) and h < 2):
                    dve.wait_ge(pt_ready[slot], 8 * (h - slot))
                dve.wait_ge(rinv_done, h + 1)
                for i in range(QT):
                    a, w = SCORE_AT[i], P * (i + 1)
                    ins = dve.tensor_scalar(ps_split[:, slot, HI, a:a + w], pr[:, slot, a:a + w],
                                            rinv[:, slot, i:i + 1], None, ALU.mult)
                ins.then_inc(p_hi, 1)

            def split_lo(h, slot):
                dve.wait_ge(p_hi, h + 1)
                for i in range(QT):
                    a, w = SCORE_AT[i], P * (i + 1)
                    ins = dve.scalar_tensor_tensor(out=ps_split[:, slot, LO, a:a + w], in0=pr[:, slot, a:a + w],
                                                   scalar=rinv[:, slot, i:i + 1], in1=ps_split[:, slot, HI, a:a + w],
                                                   op0=ALU.mult, op1=ALU.subtract)
                ins.then_inc(p_split, 1)

            def q_low(bank, h, slot):
                dve.wait_ge(q_hi, h + 1)
                dve.tensor_tensor(qT[:, slot, LO, :], gen[bank][:, :], qT[:, slot, HI, :],
                                  ALU.subtract).then_inc(q_ready, 1)

            def k_low(bank, it):
                dve.wait_ge(k_hi, it + 1)
                dve.tensor_tensor(kT[:, LO, :], gen[bank][:, :], kT[:, HI, :], ALU.subtract).then_inc(k_ready, 1)

            def v_low(bank, it):
                dve.wait_ge(v_hi, it + 1)
                dve.tensor_tensor(vT[:, LO, :], gen[bank][:, :], vT[:, HI, :], ALU.subtract).then_inc(v_ready, 1)

            def o_low(h, it, r):
                dve.wait_ge(o_hi, h + 1)
                o = oT[:, bass.ds(it % 2, 1), r]
                dve.tensor_tensor(o[:, :, LO], att[r % 2][:, :].unsqueeze(1), o[:, :, HI], ALU.subtract).then_inc(o_ready, 1)

            def add_out(bank, it, t):
                dve.wait_ge(out_filled, QT * it + t + 1)
                a = acc[:, bass.ds((it % B) * QT + t, 1), :].rearrange("p e n -> p (e n)")
                dve.scalar_tensor_tensor(out=a, in0=gen[bank][:, :], scalar=out_scale[:, 0:1], in1=a,
                                         op0=ALU.mult, op1=ALU.add).then_inc(out_added, 1)

            for i in range(len(FIRST)):
                first_low(i)
            for k in range(RING):
                dve.wait_ge(y_free[k], 16 * (NS // RING + 1))
            weights_lo(0, 3, 4, 0)
            k_low(0, 0)
            q_low(1, 0, 0)
            q_low(2, 1, 1)
            mask_rows(0, 0)
            for i in range(len(NEXT)):
                first_low(len(FIRST) + i)
            q_low(0, 2, 0)
            mask_rows(1, 1)
            split_hi(0, 0)
            split_lo(0, 0)

            def pair(it, first=False, last=False):
                for r in range(R):
                    n = it * R + r
                    scores = not (last and r >= 2)
                    more = not (last and r == R - 1)
                    if scores:
                        mask_rows(n + 2, r % 2, (0, 1))
                    if more:
                        split_hi(n + 1, (r + 1) % 2)
                    if r == 3 and not first:
                        dve.wait_ge(ffn_added, it + 1)
                        add_out(OUT_BANK[2], it - 1, 2)
                    if r != 3 and not (last and r >= 1):
                        q_low(Q_BANK[r], n + 3, (r + 1) % 2)
                    if scores:
                        mask_rows(n + 2, r % 2, (2,))
                    if r == 0:
                        v_low(V_BANK, it)
                    if more:
                        split_lo(n + 1, (r + 1) % 2)
                    if r == 1 and not last:
                        k_low(K_BANK, it + 1)
                    if r == 3 and not last:
                        q_low(Q_BANK[r], n + 3, (r + 1) % 2)
                    if r == 1 and not first:
                        add_out(OUT_BANK[0], it - 1, 0)
                    if not (first and r == 0):
                        o_low(n - 1, it if r else it - 1, (r - 1) % R)
                    if r == 2 and not first:
                        add_out(OUT_BANK[1], it - 1, 1)
                    if r == 2:
                        add_ffn(it, first)
                    if r == 3 and not last:
                        weights_lo(it + 1, it + 5, it + 5, it + 3)
                    if r == 3 and not first:
                        add_out(OUT_BANK[3], it - 1, 3)

            pair(0, first=True)
            with dve.Fori(1, NIT - 1) as it:
                pair(it)
            pair(NIT - 1, last=True)
            o_low(NH - 1, NIT - 1, R - 1)
            for t in range(QT):
                add_out(TAIL_BANK[t], NIT - 1, t)

        @block.tensor
        def _(pe):
            def products(dst, pairs):
                n = len(pairs)
                for i, (stat, mov) in enumerate(pairs):
                    for m, (a, b) in enumerate(PARTS):
                        ins = pe.matmul(dst, stat(a), mov(b), start=(i == 0 and m == 0),
                                        stop=(i == n - 1 and m == len(PARTS) - 1))
                return ins

            pe.wait_ge(consts, 12)

            def gate(t):
                pe.wait_ge(xt_done, t + 1)
                for k in range(KT):
                    for a in (HI, LO):
                        for b in (HI, LO):
                            ins = pe.matmul(gen[0][:, t * NE:(t + 1) * NE], xt[:, a, k, t * P:(t + 1) * P], wg[:, b, k, :],
                                            start=(k == 0 and a == HI and b == HI),
                                            stop=(k == KT - 1 and a == LO and b == LO))
                return ins

            for t in range(NT):
                pe.wait_ge(xhi_done, t + 1)
                pe.wait_ge(xlo_done, t + 1)
                if t >= 2:
                    pe.wait_ge(xt_done, t - 1)
                for s in (HI, LO):
                    for k in range(KT):
                        c = (s * KT + k) * P
                        ins = pe.transpose(tra[t % 2][:, c:c + P], xs[:, t % 4, s, k * P:(k + 1) * P], ident[:, :])
                ins.then_inc(xt_filled, 1)
                if t == NT // 2:
                    pe.wait_ge(wg_done, 1)
                if t >= NT // 2:
                    gate(2 * t - NT)
                    ins = gate(2 * t - NT + 1)
            ins.then_inc(gate_filled, 1)

            pe.wait_ge(chosen_done, 1)
            width = (NT + 1) * NE
            flat = chosen[:, :, :].rearrange("p t e -> p (t e)")
            pe.matmul(gen[1][:, 0:width], before[:, :], flat, start=True, stop=False, skip_group_check=True)
            for t in range(NT):
                ins = pe.matmul(gen[1][:, (t + 1) * NE:width], ones[:, :],
                                chosen[:, t:t + 1, :].broadcast_to([P, NT - t, NE]),
                                start=False, stop=(t == NT - 1), skip_group_check=True)
            ins.then_inc(rank_filled, 1)
            for j in range(TOP * NT):
                pe.wait_ge(hot_done, j + 1)
                pe.matmul(gen[0][:, 0:NS], hot_row[:, j % 4, :], hot_tile[:, j % 4, :], start=(j == 0),
                          stop=(j == TOP * NT - 1)).then_inc(hot_used, 1)

            def slot_rows(u, k):
                i = RING * u + k
                pe.wait_ge(xg_loaded[k], 16 * (u + 1))
                pe.wait_ge(xgT_free, i + 1)
                for c in range(2 * KT):
                    ins = pe.transpose(xbank[k][:, c * P:(c + 1) * P], xg[:, k, c * P:(c + 1) * P], ident[:, :])
                ins.then_inc(xg_filled, 1)

            def expert_product(u, k):
                i = RING * u + k
                e = pe.value_load(expi[0:1, bass.ds(i, 1)], min_val=0, max_val=NE - 1)
                pe.wait_ge(xgT_free, i + 1 + RING)
                pe.wait_ge(ybank_free, i + 1)
                products(ybank[k][:, :],
                         [(lambda a, c=c: xgT[:, k, a, c, :],
                           lambda b, c=c: we[:, bass.ds(e, 1), b, c * D:(c + 1) * D]) for c in range(KT)]
                         ).then_inc(y_filled, 1)

            pe.wait_ge(routed, 1)
            pe.wait_ge(we_done, NE)
            slot_rows(0, 0)
            with pe.Fori(0, NS // RING - 1) as u:
                for k in range(RING):
                    slot_rows(u + (k + 1) // RING, (k + 1) % RING)
                    expert_product(u, k)
            for k in range(RING):
                if k + 1 < RING:
                    slot_rows(NS // RING - 1, k + 1)
                expert_product(NS // RING - 1, k)

            def tokens(part, k, it, lo=0, n=S):
                return xt[:, part, k, bass.ds((it % B) * S + lo, n)]

            def fill_q(bank, h, it, r):
                w = bass.ds(((it // B) % 2) * R + r, 1)
                products(gen[bank][:, :], [(lambda a, k=k: wq[:, w, a, k, :], lambda b, k=k: tokens(b, k, it))
                                           for k in range(KT)]).then_inc(q_filled, 1)

            def fill_k(bank, it):
                w = bass.ds((it // B) % 2, 1)
                products(gen[bank][:, :], [(lambda a, k=k: wk[:, w, k, a, :], lambda b, k=k: tokens(b, k, it))
                                           for k in range(KT)]).then_inc(k_filled, 1)

            def fill_v(bank, it):
                w = bass.ds((it // B) % 2, 1)
                products(gen[bank][:, :], [(lambda a, k=k: wv[:, w, k, a, :], lambda b, k=k: tokens(b, k, it))
                                           for k in range(KT)]).then_inc(v_filled, 1)

            def fill_scores(h, slot, fills=(0, 1, 2)):
                if 0 in fills:
                    pe.wait_ge(q_ready, h + 1)
                for u in fills:
                    tiles = SCORE_FILLS[u]
                    if not (isinstance(h, int) and h == 0):
                        pe.wait_ge(s_masked, 3 * h + u - 2)
                    at = 0
                    for i in tiles:
                        w = P * (i + 1)
                        ins = products(sco[u][:, at:at + w],
                                       [(lambda a: qT[:, slot, a, i * P:(i + 1) * P], lambda b: kT[:, b, 0:w])])
                        at += w
                    ins.then_inc(s_filled, 1)

            def fill_o(h, slot):
                pe.wait_ge(pt_ready[slot], 8 * (h - slot + 2))
                if not (isinstance(h, int) and h < 2):
                    pe.wait_ge(o_ready, h - 1)
                def blocks(part, j, lo, n):
                    if n == 1:
                        return pT[:, slot, part, SCORE_AT[lo] + j * P:SCORE_AT[lo] + (j + 1) * P]
                    step = SCORE_AT[lo + 1] - SCORE_AT[lo]
                    rows = pT[:, slot, part, SCORE_AT[lo]:SCORE_AT[lo] + 2 * step].rearrange("p (i c) -> p i c", i=2)
                    return rows[:, :, j * P:(j + 1) * P]

                for j in range(QT):
                    for m, (a, b) in enumerate(PARTS):
                        for lo, n in {0: ((0, 2), (2, 2)), 1: ((1, 1), (2, 2)), 2: ((2, 2),), 3: ((3, 1),)}[j]:
                            ins = pe.matmul(att[slot][:, lo * P:(lo + n) * P], vs[:, a, j, :], blocks(b, j, lo, n),
                                            start=(j == 0 and m == 0 and lo == 0), stop=(j == lo + n - 1 and m == len(PARTS) - 1),
                                            skip_group_check=True)
                ins.then_inc(o_filled, 1)

            def fill_out(bank, it, t):
                if t == 0:
                    pe.wait_ge(o_ready, R * it + R)
                w = (it // B) % 2
                products(gen[bank][:, :],
                         [(lambda a, r=r: oT[:, bass.ds(it % 2, 1), r, a, t * P:(t + 1) * P],
                           lambda b, r=r: wo[:, bass.ds(w * R + r, 1), b, :]) for r in range(R)]).then_inc(out_filled, 1)

            pe.wait_ge(first_ready, 1)
            fill_k(0, 0)
            pe.wait_ge(first_ready, 2)
            fill_q(1, 0, 0, 0)
            pe.wait_ge(first_ready, 3)
            fill_q(2, 1, 0, 1)
            pe.wait_ge(k_ready, 1)
            pe.wait_ge(ybank_free, NS + RING)
            fill_scores(0, 0)
            pe.wait_ge(first_ready, 5)
            fill_q(0, 2, 0, 2)
            fill_scores(1, 1)
            pe.wait_ge(w_ready, 1)

            def pair(it, first=False, last=False):
                for r in range(R):
                    n = it * R + r
                    if r == 2 and not last:
                        pe.wait_ge(k_ready, it + 2)
                    if not (last and r >= 2):
                        fill_scores(n + 2, r % 2, (0, 1))
                    if r == 1:
                        if first:
                            pe.wait_ge(first_ready, len(FIRST) + len(NEXT))
                        else:
                            pe.wait_ge(w_ready, it + 1)
                    if r == 3 and not first:
                        pe.wait_ge(out_added, QT * (it - 1) + 1)
                        fill_out(OUT_BANK[2], it - 1, 2)
                    if r != 3 and not (last and r >= 1):
                        fill_q(Q_BANK[r], n + 3, it + (r > 0), (r + 3) % R)
                    if r == 0:
                        pe.wait_ge(s_masked, 3 * (n + 2) + 1)
                        fill_v(V_BANK, it)
                    if not (last and r >= 2):
                        fill_scores(n + 2, r % 2, (2,))
                    if r == 1 and not last:
                        fill_k(K_BANK, it + 1)
                    if r == 3 and not last:
                        fill_q(Q_BANK[r], n + 3, it + 1, (r + 3) % R)
                    if r == 1:
                        if not first:
                            pe.wait_ge(v_ready, it + 1)
                            fill_out(OUT_BANK[0], it - 1, 0)
                        pe.wait_ge(vs_ready, 16 * (it + 1))
                    if not (first and r == 0):
                        fill_o(n - 1, (r + 1) % 2)
                    if r == 2 and not first:
                        fill_out(OUT_BANK[1], it - 1, 1)
                    if r == 3 and not first:
                        pe.wait_ge(out_added, QT * (it - 1) + 3)
                        fill_out(OUT_BANK[3], it - 1, 3)

            pair(0, first=True)
            with pe.Fori(1, NIT - 1) as it:
                pair(it)
            pair(NIT - 1, last=True)
            fill_o(NH - 1, 1)
            for t in range(QT):
                if t >= 2:
                    pe.wait_ge(out_added, QT * (NIT - 1) + t - 2)
                fill_out(TAIL_BANK[t], NIT - 1, t)


Q_BANK = (0, 2, 2, 2)
K_BANK = 0
V_BANK = 1
OUT_BANK = (1, 0, 1, 1)
TAIL_BANK = (2, 0, 1, 2)


_INS = ['L0_attn_hidden_states', 'L0_attn_w_q', 'L0_attn_w_k', 'L0_attn_w_v', 'L0_attn_w_o', 'L0_ffn_W_gate',
        'L0_ffn_b_gate', 'L0_ffn_W_e', 'L0_ffn_b_e']


def kernel(**inputs):
    import numpy as _np
    import concourse.bacc as _bacc
    from concourse import mybir as _mybir
    from concourse.bass_utils import run_bass_kernel_spmd as _run

    nc = _bacc.Bacc("TRN2", target_bir_lowering=False, num_devices=1)
    arrays, args = {}, []
    for name in _INS:
        a = _np.ascontiguousarray(inputs[name])
        arrays[f"in_{name}_dram"] = a
        args.append(nc.dram_tensor(f"in_{name}_dram", a.shape, _mybir.dt.from_np(a.dtype), kind="ExternalInput").ap())
    shape = inputs[_INS[0]].shape
    args.append(nc.dram_tensor("out_0_dram", shape, F32, kind="ExternalOutput").ap())
    attention_moe(nc, *args)
    r = _run(nc, [arrays], core_ids=[0])
    return r.results[0]["out_0_dram"]
```

```python
from contextlib import ExitStack

import concourse.bass as bass
from concourse import mybir

ALU = mybir.AluOpType
ACT = mybir.ActivationFunctionType
AX_X = mybir.AxisListType.X
F32 = mybir.dt.float32
F16 = mybir.dt.float16
I32 = mybir.dt.int32
U32 = mybir.dt.uint32
ABSMAX = bass.bass_isa.ReduceOp.absmax

P = 128
HEAD = 128
EPS = 1e-5
MASKED = -3.0e38
LOWEST = -3.4e38
TOP = 2
HI, LO = 0, 1
PARTS = ((HI, HI), (HI, LO), (LO, HI))


def attention_moe(nc, x, w_q, w_k, w_v, w_o, w_gate, b_gate, w_e, b_e, out):
    B, S, D = x.shape
    T = B * S
    NT = T // P
    KT = D // P
    NKV = w_k.shape[1] // HEAD
    NQ = w_q.shape[1] // HEAD
    R = NQ // NKV
    NE = w_gate.shape[1]
    QT = S // P
    NIT = NKV * B
    NH = NIT * R
    NS = (TOP * T + NE * (P - 1)) // P
    RING = 3
    EARLY_SCANS = 2
    SCANS = EARLY_SCANS + 2 * (NS // RING - 1)
    POOL_EXPERTS = range(3, 7)
    assert (P, KT, R, QT, B, NE, NS % RING, SCANS) == (128, 4, 4, 4, 4, 8, 0, 26)

    SCORE_AT = [P * i * (i + 1) // 2 for i in range(QT)]
    SCORE_FILLS = ((3,), (2, 0), (1,))
    CAUSAL = P * QT * (QT + 1) // 2

    ctx = ExitStack()
    with ctx:
        def sb(name, shape, dt, where=ctx):
            return where.enter_context(nc.sbuf_tensor(name, shape, dt))

        def pb(name, shape, dt):
            return ctx.enter_context(nc.psum_tensor(name, shape, dt))

        def sem(name):
            return ctx.enter_context(nc.semaphore(name))

        acc = sb("acc", [P, NT, D], F32)
        xt = sb("xt", [P, 2, KT, T], F16)
        wst = sb("wst", [P, 1280], F32)
        wst_q = wst[:, 0:512].rearrange("p (k c) -> p k c", k=KT)
        wst_o = wst[:, 512:1024]
        wst_k = wst[:, 1024:1152]
        wst_v = wst[:, 1152:1280]
        wring = sb("wring", [P, 12288], F16)
        wq = wring[:, 0:8192].rearrange("p (h s k c) -> p h s k c", h=2 * R, s=2, k=KT)
        wk = wring[:, 8192:10240].rearrange("p (h k s c) -> p h k s c", h=2, k=KT, s=2)
        wv = wring[:, 10240:12288].rearrange("p (h k s c) -> p h k s c", h=2, k=KT, s=2)
        ident = sb("ident", [P, P], F16)
        causal = sb("causal", [P, S], F32)
        slotu = sb("slotu", [P, TOP * NT], U32)
        ystage = sb("ystage", [P, 2048], F32)
        yg = ystage[:, 0:2 * D].rearrange("p (r d) -> p r d", r=2)
        wmax = sb("wmax", [P, 4, SCANS], F32)
        carrier = sb("carrier", [P, 2, 3], F32)
        wmax4 = sb("wmax4", [P, 4], F32)
        wall4 = sb("wall4", [P, 4], F32)
        wpow = sb("wpow", [P, 4], F32)
        winv = sb("winv", [P, 4], F32)
        wscale = sb("wscale", [P, 4], F32)
        score_scale = sb("score_scale", [P, 1], F32)
        neg_score_scale = sb("neg_score_scale", [P, 1], F32)
        out_scale = sb("out_scale", [P, 1], F32)
        tmp1 = sb("tmp1", [P, 2], F32)
        table = sb("table", [P, 2], F32)

        early = ExitStack()
        we = sb("we", [P, NE, 2, KT * D], F16, early)
        be = sb("be", [P, NE, D], F32, early)
        scan = sb("scan", [P, 2560], F32, early)
        xn = sb("xn", [P, 2, D], F32, early)
        xs = sb("xs", [P, 4, 2, D], F16, early)
        xg = wring[:, 0:3072].rearrange("p (r n) -> p r n", r=RING)
        y = wring[:, 4096:7168].bitcast(F32).rearrange("p (r d) -> p r d", r=RING)
        xgT = [wring[:, a:a + 1024].rearrange("p (s k c) -> p s k c", s=2, k=KT) for a in (3072, 9216, 7168)]
        w32 = wring[:, :].bitcast(F32)
        be_flat = be[:, :, :].rearrange("p e n -> p (e n)")
        stage = [w32[:, 0:2048], w32[:, 2048:4096], scan[:, 0:2048], be_flat[:, 0:2048],
                 we[:, NE - 1].rearrange("p s n -> p (s n)").bitcast(F32), be_flat[:, 2048:4096],
                 w32[:, 4096:6144], ystage[:, :]]
        logits = wst[:, 0:128].rearrange("p (t e) -> p t e", t=NT)
        top8 = wst[:, 128:256].rearrange("p (t e) -> p t e", t=NT)
        top8i = wst[:, 256:384].bitcast(U32).rearrange("p (t e) -> p t e", t=NT)
        is1 = wst[:, 384:512].rearrange("p (t e) -> p t e", t=NT)
        is2 = wst[:, 512:640].rearrange("p (t e) -> p t e", t=NT)
        hot_tile = wst[:, 0:TOP * NT * NS // 2].bitcast(F16).rearrange("p (j n) -> p j n", n=NS)
        hot_row = wst[:, 640:896].bitcast(F16).rearrange("p (r c) -> p r c", r=4)
        past = wst[:, 896:896 + NS * NE].rearrange("p (n e) -> p n e", n=NS)
        bn = sb("bn", [P, QT, 6], F32, early)
        mv = sb("mv", [P, NT, 2], F32, early)
        std = sb("std", [P, NT], F32, early)
        rstd = sb("rstd", [P, NT], F32, early)
        nmr = sb("nmr", [P, NT], F32, early)
        eps = sb("eps", [P, 1], F32, early)
        wg32 = sb("wg32", [P, KT, NE], F32, early)
        wg = sb("wg", [P, 2, KT, NE], F16, early)
        bg = sb("bg", [P, NE], F32, early)
        iota8 = sb("iota8", [P, NE], F32, early)
        iotap = sb("iotap", [P, P], F16, early)
        iotas = sb("iotas", [P, NS], F32, early)
        iotan = sb("iotan", [P, NS], F32, early)
        token = sb("token", [P, NT], F32, early)
        before = scan[:, 2048:2112].bitcast(F16)
        ones = scan[:, 2112:2176].bitcast(F16)

        after = xn[:, :, :].rearrange("p r d -> p (r d)")
        taken = [0]

        def in_xn(n, dt=F32):
            a = after[:, taken[0]:taken[0] + n]
            taken[0] += n
            return a.bitcast(dt)

        slot_all = in_xn(NT * NE).rearrange("p (t e) -> p t e", t=NT)
        top2 = in_xn(NT * TOP).rearrange("p (t k) -> p t k", t=NT)
        slotf, rowf, tilef = in_xn(NT * TOP), in_xn(NT * TOP), in_xn(NT * TOP)
        sloti, rowi, tilei = in_xn(NT * TOP, I32), in_xn(NT * TOP, I32), in_xn(NT * TOP, I32)
        chosen = in_xn((NT + 1) * NE // 2, F16).rearrange("p (t e) -> p t e", t=NT + 1)
        cnt, tiles_ = in_xn(NE, I32), in_xn(NE, I32)
        room = in_xn(2 * (4 + NE)).rearrange("p (r n) -> p r n", r=2)
        size, base = in_xn(NE), in_xn(NE)
        expf, expi = in_xn(NS), in_xn(NS, I32)
        source = in_xn(NS, U32)
        assert taken[0] <= 2 * D
        escales = sb("escales", [P, 6, NE + 1], F32, early)
        emax, eall, epow, einv, escale, eundo = (escales[:, i, :] for i in range(6))
        early.close()

        wo = sb("wo", [P, 2 * R, 2, D], F16)
        stage_w = sb("stage_w", [P, 3 * 512], F32)
        kT = sb("kT", [P, 2, S], F16)
        vT = sb("vT", [P, 2, S], F16)
        vs = sb("vs", [P, 2, QT, HEAD], F16)
        qT = sb("qT", [P, 2, 2, S], F16)
        pr = sb("pr", [P, 2, CAUSAL], F32)
        ps_split = sb("ps_split", [P, 2, 2, CAUSAL], F16)
        pT = sb("pT", [P, 2, 2, CAUSAL], F16)
        oT = sb("oT", [P, 2, R, 2, S], F16)
        rowmax = sb("rowmax", [P, 2, QT], F32)
        negmax = sb("negmax", [P, 2, QT], F32)
        rowsum = sb("rowsum", [P, 2, QT], F32)
        rinv = sb("rinv", [P, 2, QT], F32)

        gen = [pb(f"gen{i}", [P, 512], F32) for i in range(3)]
        sco = [pb(f"sco{i}", [P, 512], F32) for i in range(3)]
        att = [pb(f"att{i}", [P, 512], F32) for i in range(2)]
        tra = [sco[i][:, :].bitcast(F16) for i in range(2)]
        ybank = sco
        xbank = [bank[:, :].bitcast(F16) for bank in (gen[2], att[0], att[1])]

        x_begun = sem("x_begun")
        x_loaded = [sem(f"x_loaded{b}") for b in range(B)]
        gate_loaded = sem("gate_loaded")
        we_loaded = [sem(f"we_loaded{e}") for e in range(NE)]
        be_loaded = sem("be_loaded")
        scan_loaded = [sem(f"scan_loaded{i}") for i in range(2)]
        first_loaded = sem("first_loaded")
        w_loaded = sem("w_loaded")
        next_loaded = sem("next_loaded")
        stored = sem("stored")
        consts = sem("consts")
        dve_chain = sem("dve_chain")
        stats_done = sem("stats_done")
        std_done = sem("std_done")
        rstd_done = sem("rstd_done")
        xn_done = sem("xn_done")
        xhi_done = sem("xhi_done")
        xlo_done = sem("xlo_done")
        xrow_stored = [sem(f"xrow_stored{i}") for i in range(4)]
        xt_filled = sem("xt_filled")
        xt_done = sem("xt_done")
        emax_done = sem("emax_done")
        eall_done = sem("eall_done")
        escale_done = sem("escale_done")
        wghi_done = sem("wghi_done")
        wg_done = sem("wg_done")
        we_hi = sem("we_hi")
        we_scaled = sem("we_scaled")
        pool_experts, dve_experts = sem("pool_experts"), sem("dve_experts")
        gate_filled = sem("gate_filled")
        chosen_done = sem("chosen_done")
        rank_filled = sem("rank_filled")
        hot_done = sem("hot_done")
        hot_used = sem("hot_used")
        source_ready = sem("source_ready")
        routed = sem("routed")
        xg_loaded = [sem(f"xg_loaded{i}") for i in range(RING)]
        xg_filled = sem("xg_filled")
        xgT_free = sem("xgT_free")
        y_filled = sem("y_filled")
        ybank_free = sem("ybank_free")
        relu_done = sem("relu_done")
        y_free = [sem(f"y_free{i}") for i in range(RING)]
        yg_loaded = sem("yg_loaded")
        ffn_added = sem("ffn_added")
        scan_free = sem("scan_free")
        wmax_done = sem("wmax_done")
        wall_done = sem("wall_done")
        wscale_done = sem("wscale_done")
        first_hi = sem("first_hi")
        first_ready = sem("first_ready")
        w_hi = sem("w_hi")
        w_ready = sem("w_ready")
        q_filled, q_hi, q_ready = sem("q_filled"), sem("q_hi"), sem("q_ready")
        k_filled, k_hi, k_ready = sem("k_filled"), sem("k_hi"), sem("k_ready")
        v_filled, v_hi, v_ready = sem("v_filled"), sem("v_hi"), sem("v_ready")
        s_filled = sem("s_filled")
        s_masked = sem("s_masked")
        bias_ready = sem("bias_ready")
        exp_done = sem("exp_done")
        rinv_done = sem("rinv_done")
        p_hi = sem("p_hi")
        p_split = sem("p_split")
        pt_ready = [sem(f"pt_ready{i}") for i in range(2)]
        vs_ready = sem("vs_ready")
        sp_steps = sem("sp_steps")
        o_filled, o_hi, o_ready = sem("o_filled"), sem("o_hi"), sem("o_ready")
        out_filled, out_added = sem("out_filled"), sem("out_added")

        x_v = x.rearrange("b (t p) d -> b p t d", p=P)
        out_v = out.rearrange("b (t p) d -> b p t d", p=P)
        wq_v = w_q.rearrange("(k p) c -> p k c", p=P)
        wk_v = w_k.rearrange("(k p) c -> p k c", p=P)
        wv_v = w_v.rearrange("(k p) c -> p k c", p=P)
        wo_v = w_o.rearrange("(h p) n -> p h n", p=P)
        xrows = nc.dram_tensor("xrows", [T, 2 * D], F16, kind="Internal").ap()
        yrows = nc.dram_tensor("yrows", [NS * P, D], F32, kind="Internal").ap()
        scan_v = [(w.rearrange("(p a) n -> p (a n)", p=P), w.shape[0] * w.shape[1] // P // 32,
                   w.shape[0] * w.shape[1] // P * (32 - EARLY_SCANS) // 32 // (SCANS - EARLY_SCANS))
                  for w in (w_q, w_k, w_v, w_o)]
        SCAN_AT = [sum(n for _, _, n in scan_v[:i]) for i in range(4)]
        scan_buffers = [xs[:, :, :, :].rearrange("p r s d -> p (r s d)").bitcast(F32), scan]

        def scanned(i, buffer, early):
            return scan_buffers[buffer][:, SCAN_AT[i]:SCAN_AT[i] + scan_v[i][1 if early else 2]]

        def wait_experts(engine):
            engine.wait_ge(pool_experts, len(POOL_EXPERTS))
            engine.wait_ge(dve_experts, NE - len(POOL_EXPERTS))

        FIRST = [(scan[:, 512 * i:512 * (i + 1)].rearrange("p (k c) -> p k c", k=KT),
                  view[:, :, h * HEAD:(h + 1) * HEAD], dst, m)
                 for i, (view, h, dst, m) in enumerate(((wk_v, 0, lambda s: wk[:, 0, :, s, :], 1),
                                                        (wq_v, 0, lambda s: wq[:, 0, s], 0),
                                                        (wq_v, 1, lambda s: wq[:, 1, s], 0),
                                                        (wq_v, 2, lambda s: wq[:, 2, s], 0),
                                                        (wv_v, 0, lambda s: wv[:, 0, :, s, :], 2)))]

        NEXT = [(stage_w[:, 0:512].rearrange("p (k c) -> p k c", k=KT), wq_v[:, :, 4 * HEAD:5 * HEAD],
                 lambda s: wq[:, 4, s], 0)]
        NEXT += [(stage_w[:, 512 * i:512 * (i + 1)], wo_v[:, i, :], lambda s, i=i: wo[:, i, s, :], 3) for i in (1, 2)]

        block = ctx.enter_context(nc.Block())

        @block.sync
        def _(sp):
            sp.dma_start(acc[:, 0:2, :], x_v[0][:, 0:2, :]).then_inc(x_begun, 16)
            for b in range(B):
                t0 = 0 if b else 2
                sp.dma_start(acc[:, b * QT + t0:(b + 1) * QT, :], x_v[b][:, t0:, :]).then_inc(x_loaded[b], 16)
                if b == 0:
                    sp.dma_start(wg32[:, :, :], w_gate.rearrange("(k p) e -> p k e", p=P)).then_inc(gate_loaded, 16)
                    sp.dma_start(bg[:, :], b_gate.partition_broadcast(P)).then_inc(gate_loaded, 16)

            def load_expert(e):
                sp.dma_start(stage[e].rearrange("p (k n) -> p k n", k=KT),
                             w_e[e].rearrange("(k p) n -> p k n", p=P)).then_inc(we_loaded[e], 16)

            load_expert(0)
            for t in range(NT):
                sp.wait_ge(xlo_done, t + 1)
                sp.dma_start(xrows[t * P:(t + 1) * P, :],
                             xs[:, t % 4].rearrange("p s d -> p (s d)")).then_inc(xrow_stored[t % 4], 16)
                if t % 2 and t // 2 + 1 < NE:
                    load_expert(t // 2 + 1)

            def load_scan(c, buffer, early=False):
                sp.wait_ge(scan_free, c + 1)
                for i, (view, n0, n) in enumerate(scan_v):
                    cols = bass.ds(c * n0, n0) if early else bass.ds(c * n + EARLY_SCANS * (n0 - n), n)
                    sp.dma_start(scanned(i, buffer, early), view[:, cols]).then_inc(scan_loaded[buffer], 16)

            def store_y(u, k):
                sp.wait_ge(relu_done, RING * u + k + 1)
                sp.dma_start(yrows[bass.ds((RING * u + k) * P, P), :], y[:, k, :]).then_inc(y_free[k], 16)

            for i in range(4):
                sp.wait_ge(xrow_stored[i], 16 * NT // 4)
            sp.wait_ge(rank_filled, 1)
            load_scan(0, 0, early=True)
            sp.wait_ge(pool_experts, 3)
            sp.dma_start(be[:, :, :], b_e.partition_broadcast(P)).then_inc(be_loaded, 16)
            sp.wait_ge(dve_experts, 3)
            load_scan(1, 1, early=True)
            load_scan(2, 0)
            load_scan(3, 1)

            with sp.Fori(0, NS // RING - 2) as u:
                store_y(u, 0)
                store_y(u, 1)
                load_scan(2 * u + EARLY_SCANS + 2, 0)
                store_y(u, 2)
                load_scan(2 * u + EARLY_SCANS + 3, 1)
            for k in range(RING):
                store_y(NS // RING - 2, k)
            sp.wait_ge(scan_free, SCANS + 2)
            for where, src, _, _ in FIRST:
                sp.dma_start(where, src).then_inc(first_loaded, 16)

            def load_piece(q, kv, o):
                sp.dma_start(wst_q, wq_v[:, :, bass.ds(q * HEAD, HEAD)]).then_inc(w_loaded, 16)
                block, col = bass.ds(kv % KT, 1), bass.ds((kv // R) * HEAD, HEAD)
                sp.dma_start(wst_k, wk_v[:, block, col]).then_inc(w_loaded, 16)
                sp.dma_start(wst_v, wv_v[:, block, col]).then_inc(w_loaded, 16)
                sp.dma_start(wst_o, wo_v[:, bass.ds(o, 1), :]).then_inc(w_loaded, 16)

            load_piece(3, 4, 0)
            for k in range(RING):
                store_y(NS // RING - 1, k)
            sp.wait_ge(ybank_free, NS + RING)
            for where, src, _, _ in NEXT:
                sp.dma_start(where, src).then_inc(next_loaded, 16)

            def transpose_p(h, slot):
                sp.wait_ge(p_split, h + 1)
                sp.sem_inc(sp_steps, 1)
                if not (isinstance(h, int) and h < 2):
                    sp.wait_ge(o_filled, h - 1)
                    sp.sem_inc(sp_steps, 1)
                sp.dma_start(pT[:, slot].rearrange("p s (b c) -> p (s b) c", c=P),
                             ps_split[:, slot].rearrange("p s c -> p (s c)"),
                             transpose=True).then_inc(pt_ready[slot], 16)

            def transpose_v(it):
                sp.wait_ge(v_ready, it + 1)
                sp.sem_inc(sp_steps, 1)
                if not (isinstance(it, int) and it == 0):
                    sp.wait_ge(o_filled, R * it)
                    sp.sem_inc(sp_steps, 1)
                sp.dma_start(vs[:, :, :, :].rearrange("p s t d -> p (s t) d"),
                             vT[:, :, :].rearrange("p s c -> p (s c)"), transpose=True).then_inc(vs_ready, 16)

            def pair(it, last=False):
                for r in range(R):
                    if r == 0:
                        transpose_v(it)
                    if not (last and r == R - 1):
                        transpose_p(it * R + r + 1, (r + 1) % 2)
                    if r == 0 and not last:
                        sp.wait_ge(w_ready, it + 1)
                        load_piece((it + 5) % NQ, (it + 5) % NQ, (it + 3) % NQ)

            transpose_p(0, 0)
            pair(0)
            with sp.Fori(1, NIT - 1) as it:
                pair(it)
            pair(NIT - 1, last=True)
            for b in range(B - 1):
                sp.wait_ge(out_added, QT * (NIT - B + b + 1))
                sp.dma_start(out_v[b], acc[:, b * QT:(b + 1) * QT, :]).then_inc(stored, 16)
            for t in range(QT):
                sp.wait_ge(out_added, QT * (NIT - 1) + t + 1)
                sp.dma_start(out_v[B - 1][:, t, :], acc[:, (B - 1) * QT + t, :]).then_inc(stored, 16)
            sp.wait_ge(stored, 16 * (B - 1 + QT))

        @block.gpsimd
        def _(pool):
            pool.memset(ident[:, :], 0.0).then_inc(consts, 1)
            pool.memset(causal[:, :], 0.0).then_inc(consts, 1)
            pool.wait_ge(consts, 2)
            pool.affine_select(out=ident[:, :], in_=ident[:, :], compare_op=ALU.not_equal, fill=1.0, base=0,
                               pattern=[[-1, P]], channel_multiplier=1).then_inc(consts, 1)
            pool.affine_select(out=causal[:, S - P:S], in_=causal[:, S - P:S], compare_op=ALU.is_ge, fill=MASKED,
                               base=0, pattern=[[-1, P]], channel_multiplier=1).then_inc(consts, 1)
            pool.iota(iota8[:, :], pattern=[[1, NE]], base=0, channel_multiplier=0,
                      allow_small_or_imprecise_dtypes=True).then_inc(consts, 1)
            pool.iota(iotap[:, :], pattern=[[1, P]], base=0, channel_multiplier=0,
                      allow_small_or_imprecise_dtypes=True).then_inc(consts, 1)
            pool.iota(iotas[:, :], pattern=[[P, NS]], base=0, channel_multiplier=0,
                      allow_small_or_imprecise_dtypes=True).then_inc(consts, 1)
            pool.iota(iotan[:, :], pattern=[[1, NS]], base=0, channel_multiplier=0,
                      allow_small_or_imprecise_dtypes=True).then_inc(consts, 1)
            pool.iota(token[:, :], pattern=[[P, NT]], base=0, channel_multiplier=1,
                      allow_small_or_imprecise_dtypes=True).then_inc(consts, 1)
            pool.memset(ones[:, :], 1.0).then_inc(consts, 1)
            pool.memset(before[:, :], 0.0).then_inc(consts, 1)
            pool.wait_ge(consts, 11)
            pool.affine_select(out=before[:, :], in_=before[:, :], compare_op=ALU.is_ge, fill=1.0, base=0,
                               pattern=[[-1, P]], channel_multiplier=1).then_inc(consts, 1)

            def all_max(i):
                cols = slice(max(2 * i - 1, 0), 2 * i + 1)
                pool.wait_ge(emax_done, i + 1)
                pool.partition_all_reduce(eall[:, cols], emax[:, cols], P, ABSMAX).then_inc(eall_done, 1)

            def expert_lo(e):
                pool.wait_ge(we_scaled, POOL_EXPERTS.index(e) + 1)
                pool.tensor_tensor(we[:, e, LO, :], stage[e], we[:, e, HI, :], ALU.subtract).then_inc(pool_experts, 1)

            for i in range(4):
                all_max(i)
            expert_lo(3)
            all_max(4)
            for e in POOL_EXPERTS[1:]:
                expert_lo(e)
            pool.wait_ge(source_ready, 1)
            pool.wait_ge(pool_experts, len(POOL_EXPERTS))
            pool.wait_ge(dve_experts, 2)
            for i in range(4):
                pool.wait_ge(xrow_stored[i], 16 * NT // 4)
            for i in range(NS):
                if i >= RING:
                    pool.wait_ge(xg_filled, i - RING + 1)
                pool.indirect_dma_start(out=xg[:, i % RING, :], out_offset=None, in_=xrows,
                                        in_offset=bass.IndirectOffsetOnAxis(ap=source[:, i:i + 1], axis=0)
                                        ).then_inc(xg_loaded[i % RING], 16)
            pool.wait_ge(wmax_done, 1)
            pool.partition_all_reduce(wall4[:, :], wmax4[:, :], P, ABSMAX).then_inc(wall_done, 1)
            for k in range(RING):
                pool.wait_ge(y_free[k], 16 * (NS // RING + 1))
            for j in range(TOP * NT):
                if j:
                    pool.wait_ge(yg_loaded, 16 * j)
                if j >= 2:
                    pool.wait_ge(ffn_added, j - 1)
                pool.indirect_dma_start(out=yg[:, j % 2, :], out_offset=None, in_=yrows,
                                        in_offset=bass.IndirectOffsetOnAxis(ap=slotu[:, j:j + 1], axis=0)
                                        ).then_inc(yg_loaded, 16)

        @block.scalar
        def _(act):
            act.wait_ge(stats_done, 1)
            act.activation(table[:, 0:1], eps[:, 0:1], ACT.Sqrt, bias=eps[:, 0:1])

            def deviations(b):
                act.wait_ge(stats_done, b + 2)
                act.activation(std[:, b * QT:(b + 1) * QT], mv[:, b * QT:(b + 1) * QT, 1], ACT.Sqrt,
                               bias=eps[:, 0:1]).then_inc(std_done, 1)

            def normalise(t):
                if t % QT == 0:
                    act.wait_ge(rstd_done, t // QT + 1)
                if t >= 2:
                    act.wait_ge(xlo_done, t - 1)
                act.activation(xn[:, t % 2, :], acc[:, t, :], ACT.Identity, bias=nmr[:, t:t + 1],
                               scale=rstd[:, t:t + 1]).then_inc(xn_done, 1)
                if t >= 4:
                    act.wait_ge(xt_filled, t - 3)
                    act.wait_ge(xrow_stored[t % 4], 16 * (t // 4))
                act.wait_ge(xn_done, t + 1)
                act.activation(xs[:, t % 4, HI, :], xn[:, t % 2, :], ACT.Copy).then_inc(xhi_done, 1)

            def copy_xt(t):
                act.wait_ge(xt_filled, t + 1)
                act.activation(xt[:, :, :, t * P:(t + 1) * P],
                               tra[t % 2][:, :].rearrange("p (s k c) -> p s k c", s=2, k=KT),
                               ACT.Copy).then_inc(xt_done, 1)

            def expert_hi(e):
                act.wait_ge(escale_done, e // 2 + 2)
                if e == NE - 1:
                    act.wait_ge(pool_experts, 2)
                scale = escale[:, e + 1:e + 2]
                act.activation(we[:, e, HI, :], stage[e], ACT.Copy, scale=scale).then_inc(we_hi, 1)
                act.wait_ge(we_hi, e + 1)
                if e in POOL_EXPERTS:
                    act.activation(stage[e], stage[e], ACT.Copy, scale=scale).then_inc(we_scaled, 1)

            deviations(0)
            for t in range(NT):
                normalise(t)
                if t:
                    copy_xt(t - 1)
                if t % QT == 2 and t + QT < NT:
                    deviations(t // QT + 1)
                if t == 4:
                    act.wait_ge(escale_done, 1)
                    act.activation(wg[:, HI], wg32[:, :, :], ACT.Copy, scale=escale[:, 0:1]).then_inc(wghi_done, 1)
                if t in (9, 12, 15):
                    expert_hi((9, 12, 15).index(t))
            copy_xt(NT - 1)
            for e in range(3, NE):
                expert_hi(e)

            act.activation(table[:, 1:2], eps[:, 0:1], ACT.Exp)

            def copy_xg(u, k):
                i = RING * u + k
                act.wait_ge(xg_filled, i + 1)
                act.activation(xgT[k], xbank[k].rearrange("p (s k c) -> p s k c", s=2, k=KT),
                               ACT.Copy).then_inc(xgT_free, 1)

            def relu(u, k):
                act.wait_ge(ybank_free, RING * u + k + 1 + RING)
                act.activation(y[:, k, :], y[:, k, :], ACT.Relu, scale=0.5).then_inc(relu_done, 1)

            wait_experts(act)
            copy_xg(0, 0)
            copy_xg(0, 1)
            with act.Fori(0, NS // RING - 1) as u:
                for k in range(RING):
                    copy_xg(u + (k + 2) // RING, (k + 2) % RING)
                    relu(u, k)
            copy_xg(NS // RING - 1, 2)
            relu(NS // RING - 1, 0)
            relu(NS // RING - 1, 1)

            act.wait_ge(wscale_done, 1)

            def first_high(i):
                where, _, dst, m = (FIRST + NEXT)[i]
                act.activation(dst(HI), where, ACT.Copy, scale=wscale[:, m:m + 1]).then_inc(first_hi, 1)

            def weights_hi(piece, q, kv, o):
                act.wait_ge(w_loaded, 64 * (piece + 1))
                act.activation(wq[:, bass.ds(q % (2 * R), 1), HI], wst_q, ACT.Copy, scale=wscale[:, 0:1])
                group, block = bass.ds((kv // R) % 2, 1), bass.ds(kv % KT, 1)
                act.activation(wk[:, group, block, HI], wst_k, ACT.Copy, scale=wscale[:, 1:2])
                act.activation(wv[:, group, block, HI], wst_v, ACT.Copy, scale=wscale[:, 2:3])
                act.activation(wo[:, bass.ds(o % (2 * R), 1), HI], wst_o, ACT.Copy,
                               scale=wscale[:, 3:4]).then_inc(w_hi, 1)

            def q_high(bank, h, slot):
                act.wait_ge(q_filled, h + 1)
                act.activation(qT[:, slot, HI, :], gen[bank][:, :], ACT.Copy).then_inc(q_hi, 1)

            def k_high(bank, it):
                act.wait_ge(k_filled, it + 1)
                act.activation(kT[:, HI, :], gen[bank][:, :], ACT.Copy).then_inc(k_hi, 1)

            def v_high(bank, it):
                if not (isinstance(it, int) and it == 0):
                    act.wait_ge(vs_ready, 16 * it)
                act.wait_ge(v_filled, it + 1)
                act.activation(vT[:, HI, :], gen[bank][:, :], ACT.Copy).then_inc(v_hi, 1)

            def exps(h, slot):
                act.wait_ge(bias_ready, h + 1)
                for i in range(QT):
                    a = SCORE_AT[i]
                    row = pr[:, slot, a:a + P * (i + 1)]
                    last = act.activation(row, row, ACT.Exp, bias=negmax[:, slot, i:i + 1],
                                          scale=score_scale[:, 0:1], accum_out=rowsum[:, slot, i:i + 1])
                last.then_inc(exp_done, 1)

            def o_high(h, it, r):
                act.wait_ge(o_filled, h + 1)
                act.activation(oT[:, bass.ds(it % 2, 1), r, HI, :], att[r % 2][:, :], ACT.Copy).then_inc(o_hi, 1)

            act.wait_ge(first_loaded, 16 * len(FIRST))
            for i in range(len(FIRST)):
                first_high(i)
            relu(NS // RING - 1, 2)
            k_high(0, 0)
            q_high(1, 0, 0)
            q_high(2, 1, 1)
            weights_hi(0, 3, 4, 0)
            for k in range(RING):
                act.wait_ge(y_free[k], 16 * (NS // RING + 1))
            act.wait_ge(next_loaded, 16 * len(NEXT))
            first_high(len(FIRST))
            exps(0, 0)
            q_high(0, 2, 0)
            for i in range(1, len(NEXT)):
                first_high(len(FIRST) + i)
            exps(1, 1)

            def pair(it, first=False, last=False):
                for r in range(R):
                    n = it * R + r
                    if r != 3 and not (last and r >= 1):
                        q_high(Q_BANK[r], n + 3, (r + 1) % 2)
                    if r == 1 and not last:
                        k_high(K_BANK, it + 1)
                    if r == 3 and not last:
                        q_high(Q_BANK[r], n + 3, (r + 1) % 2)
                    if r == 0:
                        v_high(V_BANK, it)
                    if not (first and r == 0):
                        o_high(n - 1, it if r else it - 1, (r - 1) % R)
                    if not (last and r >= 2):
                        exps(n + 2, r % 2)
                    if r == 2 and not last:
                        act.wait_ge(k_filled, it + 2)
                        weights_hi(it + 1, it + 5, it + 5, it + 3)

            pair(0, first=True)
            with act.Fori(1, NIT - 1) as it:
                pair(it)
            pair(NIT - 1, last=True)
            o_high(NH - 1, NIT - 1, R - 1)

        @block.vector
        def _(dve):
            chain = [0]

            def link(ins):
                chain[0] += 1
                ins.then_inc(dve_chain, 1)
                dve.wait_ge(dve_chain, chain[0])

            def powers(allmax, pow2, inv, scale):
                link(dve.tensor_scalar(pow2, allmax, 2.0 ** -60, None, ALU.max))
                link(dve.tensor_scalar(pow2.bitcast(I32), pow2.bitcast(I32), 0x7F800000, None, ALU.bitwise_and))
                link(dve.reciprocal(inv, pow2))
                return dve.tensor_scalar(scale, inv, 8.0, None, ALU.mult)

            dve.memset(eps[:, :], EPS).then_inc(stats_done, 1)
            for k in range(RING):
                dve.memset(tmp1[:, 0:1] if k == 0 else tmp1[:, 1:2] if k == 1 else carrier[:, 0, 0:1], 0.0
                           ).then_inc(y_free[k], 16)
            dve.memset(carrier[:, 0, 1:2], 0.0).then_inc(scan_free, 2)
            dve.memset(carrier[:, 0, 2:3], 0.0).then_inc(xgT_free, RING)
            link(dve.memset(carrier[:, 1, 0:1], 0.0))

            def stats(b):
                tiles = range(b * QT, (b + 1) * QT)
                dve.wait_ge(x_loaded[b] if b else x_begun, 16)
                for t in tiles:
                    if t == 2:
                        dve.wait_ge(x_loaded[0], 16)
                    ins = dve.bn_stats(bn[:, t % QT, :], acc[:, t, :])
                link(ins)
                for t in tiles:
                    ins = dve.bn_aggr(mv[:, t, :], bn[:, t % QT, :])
                ins.then_inc(stats_done, 1)

            def inverse(b):
                cols = slice(b * QT, (b + 1) * QT)
                dve.wait_ge(std_done, b + 1)
                link(dve.reciprocal(rstd[:, cols], std[:, cols]))
                dve.scalar_tensor_tensor(out=nmr[:, cols], in0=mv[:, cols, 0], scalar=-1.0, in1=rstd[:, cols],
                                         op0=ALU.mult, op1=ALU.mult).then_inc(rstd_done, 1)

            def low(t):
                dve.wait_ge(xhi_done, t + 1)
                dve.tensor_tensor(xs[:, t % 4, LO, :], xn[:, t % 2, :], xs[:, t % 4, HI, :],
                                  ALU.subtract).then_inc(xlo_done, 1)

            def expert_max(e):
                dve.wait_ge(we_loaded[e], 16)
                ins = dve.tensor_reduce(emax[:, e + 1:e + 2], stage[e], AX_X, ALU.max, apply_absolute_value=True)
                if e % 2:
                    ins.then_inc(emax_done, 1)

            def expert_scales(i):
                cols = slice(max(2 * i - 1, 0), 2 * i + 1)
                dve.wait_ge(eall_done, i + 1)
                link(powers(eall[:, cols], epow[:, cols], einv[:, cols], escale[:, cols]))
                dve.tensor_scalar(eundo[:, cols], epow[:, cols], 0.125, None, ALU.mult).then_inc(escale_done, 1)

            def expert_low(e):
                dve.wait_ge(we_hi, e + 1)
                dve.scalar_tensor_tensor(out=we[:, e, LO, :], in0=stage[e], scalar=escale[:, e + 1:e + 2],
                                         in1=we[:, e, HI, :], op0=ALU.mult, op1=ALU.subtract).then_inc(dve_experts, 1)

            stats(0)
            inverse(0)
            for t in range(NT):
                low(t)
                if t % QT == 1 and t + QT < NT:
                    stats(t // QT + 1)
                if t % QT == 3 and t + QT < NT:
                    inverse(t // QT + 1)
                if t == 1:
                    dve.wait_ge(gate_loaded, 32)
                    dve.tensor_reduce(emax[:, 0:1], wg32[:, :, :], mybir.AxisListType.XY, ALU.max,
                                      apply_absolute_value=True).then_inc(emax_done, 1)
                if t in (3, 7, 11, 15):
                    expert_scales((3, 7, 11, 15).index(t))
                if t % 2 and t >= 3:
                    expert_max((t - 3) // 2)
                if t == 5:
                    dve.wait_ge(wghi_done, 1)
                    dve.scalar_tensor_tensor(out=wg[:, LO], in0=wg32[:, :, :], scalar=escale[:, 0:1], in1=wg[:, HI],
                                             op0=ALU.mult, op1=ALU.subtract).then_inc(wg_done, 1)
                if t in (12, 14):
                    expert_low((12, 14).index(t))
            dve.wait_ge(xlo_done, NT)
            dve.memset(room[:, :, :], 0.0)
            dve.memset(chosen[:, NT, :], 0.0)

            dve.wait_ge(gate_filled, 1)
            link(dve.scalar_tensor_tensor(out=logits[:, :, :],
                                          in0=gen[0][:, 0:NT * NE].rearrange("p (t e) -> p t e", t=NT),
                                          scalar=eundo[:, 0:1], in1=bg[:, :].unsqueeze(1).broadcast_to([P, NT, NE]),
                                          op0=ALU.mult, op1=ALU.add))
            for t in range(NT):
                ins = dve.max(top8[:, t, :], logits[:, t, :])
            link(ins)
            for t in range(NT):
                ins = dve.max_index(top8i[:, t, :], top8[:, t, :], logits[:, t, :])
            link(ins)
            link(dve.tensor_copy(top2[:, :, :], top8i[:, :, 0:TOP]))
            dve.wait_ge(consts, 12)
            all_iota = iota8[:, :].unsqueeze(1).broadcast_to([P, NT, NE])
            dve.tensor_tensor(is1[:, :, :], all_iota, top2[:, :, 0:1].broadcast_to([P, NT, NE]), ALU.is_equal)
            link(dve.tensor_tensor(is2[:, :, :], all_iota, top2[:, :, 1:2].broadcast_to([P, NT, NE]), ALU.is_equal))
            dve.tensor_tensor(chosen[:, 0:NT, :], is1[:, :, :], is2[:, :, :], ALU.add).then_inc(chosen_done, 1)
            expert_max(NE - 1)

            dve.wait_ge(rank_filled, 1)
            ranks = gen[1][:, 0:NT * NE].rearrange("p (t e) -> p t e", t=NT)
            link(dve.tensor_scalar(cnt[:, :], gen[1][:, NT * NE:(NT + 1) * NE], float(P - 1), None, ALU.add))
            link(dve.tensor_scalar(tiles_[:, :], cnt[:, :], 7, None, ALU.arith_shift_right))
            dve.tensor_scalar(size[:, :], tiles_[:, :], float(P), None, ALU.mult)
            link(dve.tensor_scalar(room[:, 0, 4:4 + NE], tiles_[:, :], float(P), None, ALU.mult))
            for i, d in enumerate((1, 2, 4)):
                link(dve.tensor_tensor(room[:, (i + 1) % 2, 4:4 + NE], room[:, i % 2, 4:4 + NE],
                                       room[:, i % 2, 4 - d:4 + NE - d], ALU.add))
            until = room[:, 1, 4:4 + NE]
            link(dve.tensor_tensor(base[:, :], until, size[:, :], ALU.subtract))
            link(dve.tensor_tensor(slot_all[:, :, :], ranks, base[:, :].unsqueeze(1).broadcast_to([P, NT, NE]),
                                   ALU.add))
            dve.tensor_tensor(is1[:, :, :], is1[:, :, :], slot_all[:, :, :], ALU.mult)
            link(dve.tensor_tensor(is2[:, :, :], is2[:, :, :], slot_all[:, :, :], ALU.mult))
            slot2 = slotf[:, :].rearrange("p (t k) -> p t k", k=TOP)
            dve.tensor_reduce(slot2[:, :, 0], is1[:, :, :], AX_X, ALU.add)
            link(dve.tensor_reduce(slot2[:, :, 1], is2[:, :, :], AX_X, ALU.add))
            dve.tensor_copy(slotu[:, :], slotf[:, :])
            link(dve.tensor_copy(sloti[:, :], slotf[:, :]))
            dve.tensor_scalar(rowi[:, :], sloti[:, :], P - 1, None, ALU.bitwise_and)
            link(dve.tensor_scalar(tilei[:, :], sloti[:, :], 7, None, ALU.arith_shift_right))
            dve.tensor_copy(rowf[:, :], rowi[:, :])
            link(dve.tensor_copy(tilef[:, :], tilei[:, :]))
            link(dve.tensor_tensor(hot_tile[:, :, :], iotan[:, :].unsqueeze(1).broadcast_to([P, TOP * NT, NS]),
                                   tilef[:, :].unsqueeze(2).broadcast_to([P, TOP * NT, NS]), ALU.is_equal))
            expert_scales(4)
            for j in range(TOP * NT):
                if j >= 4:
                    dve.wait_ge(hot_used, j - 3)
                dve.tensor_scalar(hot_row[:, j % 4, :], iotap[:, :], rowf[:, j:j + 1],
                                  token[:, j // TOP:j // TOP + 1], ALU.is_equal, ALU.mult).then_inc(hot_done, 1)
            link(dve.tensor_tensor(past[:, :, :], iotas[:, :].unsqueeze(2).broadcast_to([P, NS, NE]),
                                   until.unsqueeze(1).broadcast_to([P, NS, NE]), ALU.is_ge))
            dve.wait_ge(hot_used, TOP * NT)
            dve.tensor_copy(source[:, :], gen[0][:, 0:NS]).then_inc(source_ready, 1)
            link(dve.tensor_reduce(expf[:, :], past[:, :, :], AX_X, ALU.add))
            dve.tensor_scalar(expi[:, :], expf[:, :], float(NE - 1), None, ALU.min).then_inc(routed, 1)
            expert_low(2)
            expert_low(NE - 1)
            dve.memset(carrier[:, 1, 1:2], 0.0).then_inc(ybank_free, RING)

            def scan_max(c, turn, buffer, early=False):
                dve.wait_ge(scan_loaded[buffer], 64 * (turn + 1))
                for i in range(4):
                    ins = dve.tensor_reduce(wmax[:, i, bass.ds(c, 1)], scanned(i, buffer, early), AX_X, ALU.max,
                                            apply_absolute_value=True)
                ins.then_inc(scan_free, 1)

            def expert_out(u, k):
                i = RING * u + k
                e = dve.value_load(expi[0:1, bass.ds(i, 1)], min_val=0, max_val=NE - 1)
                dve.wait_ge(y_free[k], 16 * (u + 1))
                dve.wait_ge(y_filled, i + 1)
                dve.scalar_tensor_tensor(out=y[:, k, :], in0=ybank[k][:, :], scalar=eundo[:, bass.ds(e + 1, 1)],
                                         in1=be[:, bass.ds(e, 1), :].rearrange("p e n -> p (e n)"),
                                         op0=ALU.mult, op1=ALU.add).then_inc(ybank_free, 1)

            for c in range(EARLY_SCANS):
                scan_max(c, 0, c, early=True)
            dve.wait_ge(routed, 1)
            dve.wait_ge(escale_done, 5)
            dve.wait_ge(be_loaded, 16)
            wait_experts(dve)
            with dve.Fori(0, NS // RING - 1) as u:
                expert_out(u, 0)
                expert_out(u, 1)
                scan_max(2 * u + EARLY_SCANS, u + EARLY_SCANS // 2, 0)
                expert_out(u, 2)
                scan_max(2 * u + EARLY_SCANS + 1, u + EARLY_SCANS // 2, 1)

            dve.wait_ge(scan_free, SCANS + 2)
            dve.tensor_reduce(wmax4[:, :], wmax[:, :, :], AX_X, ALU.max).then_inc(wmax_done, 1)
            expert_out(NS // RING - 1, 0)
            dve.wait_ge(wall_done, 1)
            powers(wall4[:, :], wpow[:, :], winv[:, :], wscale[:, :]).then_inc(wscale_done, 1)
            expert_out(NS // RING - 1, 1)
            dve.wait_ge(wscale_done, 1)
            link(dve.tensor_scalar(score_scale[:, :], wpow[:, 0:1], wpow[:, 1:2], HEAD ** -0.5 / 64,
                                   ALU.mult, ALU.mult))
            dve.tensor_scalar(neg_score_scale[:, :], score_scale[:, :], -1.0, None, ALU.mult)
            link(dve.tensor_scalar(out_scale[:, :], wpow[:, 2:3], wpow[:, 3:4], 1.0 / 64, ALU.mult, ALU.mult))

            def lower(dst, src, high, m):
                return dve.scalar_tensor_tensor(out=dst, in0=src, scalar=wscale[:, m:m + 1], in1=high,
                                                op0=ALU.mult, op1=ALU.subtract)

            def first_low(i):
                where, _, dst, m = (FIRST + NEXT)[i]
                dve.wait_ge(first_hi, i + 1)
                lower(dst(LO), where, dst(HI), m).then_inc(first_ready, 1)

            def weights_lo(piece, q, kv, o):
                dve.wait_ge(w_hi, piece + 1)
                a = wq[:, bass.ds(q % (2 * R), 1)]
                lower(a[:, :, LO].rearrange("p e k c -> p (e k c)"), wst[:, 0:512],
                      a[:, :, HI].rearrange("p e k c -> p (e k c)"), 0)
                for w, src, m in ((wk, wst_k, 1), (wv, wst_v, 2)):
                    a = w[:, bass.ds((kv // R) % 2, 1), bass.ds(kv % KT, 1)]
                    lower(a[:, :, :, LO].rearrange("p a b c -> p (a b c)"), src,
                          a[:, :, :, HI].rearrange("p a b c -> p (a b c)"), m)
                a = wo[:, bass.ds(o % (2 * R), 1)]
                lower(a[:, :, LO].rearrange("p e n -> p (e n)"), wst_o,
                      a[:, :, HI].rearrange("p e n -> p (e n)"), 3).then_inc(w_ready, 1)

            def add_ffn(it, first):
                if not first:
                    dve.wait_ge(out_added, QT * (it - 1) + 2)
                dve.wait_ge(yg_loaded, 16 * it + 16)
                a = acc[:, bass.ds(it // TOP, 1), :]
                dve.tensor_tensor(a, a, yg[:, bass.ds(it % TOP, 1), :], ALU.add).then_inc(ffn_added, 1)

            def mask_rows(h, slot, fills=(0, 1, 2)):
                if not (isinstance(h, int) and h < 2) and 0 in fills:
                    dve.wait_ge(p_split, h - 1)
                for u in fills:
                    tiles = SCORE_FILLS[u]
                    dve.wait_ge(s_filled, 3 * h + u + 1)
                    dve.memset(carrier[:, slot, u:u + 1], 0.0)
                    at = 0
                    for i in tiles:
                        w = P * (i + 1)
                        a = SCORE_AT[i]
                        ins = dve.tensor_tensor_reduce(pr[:, slot, a:a + w], sco[u][:, at:at + w],
                                                       causal[:, S - w:S], 1.0, LOWEST, ALU.add, ALU.max,
                                                       rowmax[:, slot, i:i + 1])
                        at += w
                    ins.then_inc(s_masked, 1)
                if 2 not in fills:
                    return
                dve.wait_ge(s_masked, 3 * h + 3)
                dve.tensor_scalar(negmax[:, slot, :], rowmax[:, slot, :], neg_score_scale[:, 0:1], None,
                                  ALU.mult).then_inc(bias_ready, 1)

            def split_hi(h, slot):
                dve.wait_ge(exp_done, h + 1)
                dve.reciprocal(rinv[:, slot, :], rowsum[:, slot, :]).then_inc(rinv_done, 1)
                if not (isinstance(h, int) and h < 2):
                    dve.wait_ge(pt_ready[slot], 8 * (h - slot))
                dve.wait_ge(rinv_done, h + 1)
                for i in range(QT):
                    a, w = SCORE_AT[i], P * (i + 1)
                    ins = dve.tensor_scalar(ps_split[:, slot, HI, a:a + w], pr[:, slot, a:a + w],
                                            rinv[:, slot, i:i + 1], None, ALU.mult)
                ins.then_inc(p_hi, 1)

            def split_lo(h, slot):
                dve.wait_ge(p_hi, h + 1)
                for i in range(QT):
                    a, w = SCORE_AT[i], P * (i + 1)
                    ins = dve.scalar_tensor_tensor(out=ps_split[:, slot, LO, a:a + w], in0=pr[:, slot, a:a + w],
                                                   scalar=rinv[:, slot, i:i + 1], in1=ps_split[:, slot, HI, a:a + w],
                                                   op0=ALU.mult, op1=ALU.subtract)
                ins.then_inc(p_split, 1)

            def q_low(bank, h, slot):
                dve.wait_ge(q_hi, h + 1)
                dve.tensor_tensor(qT[:, slot, LO, :], gen[bank][:, :], qT[:, slot, HI, :],
                                  ALU.subtract).then_inc(q_ready, 1)

            def k_low(bank, it):
                dve.wait_ge(k_hi, it + 1)
                dve.tensor_tensor(kT[:, LO, :], gen[bank][:, :], kT[:, HI, :], ALU.subtract).then_inc(k_ready, 1)

            def v_low(bank, it):
                dve.wait_ge(v_hi, it + 1)
                dve.tensor_tensor(vT[:, LO, :], gen[bank][:, :], vT[:, HI, :], ALU.subtract).then_inc(v_ready, 1)

            def o_low(h, it, r):
                dve.wait_ge(o_hi, h + 1)
                o = oT[:, bass.ds(it % 2, 1), r]
                dve.tensor_tensor(o[:, :, LO], att[r % 2][:, :].unsqueeze(1), o[:, :, HI],
                                  ALU.subtract).then_inc(o_ready, 1)

            def add_out(bank, it, t):
                dve.wait_ge(out_filled, QT * it + t + 1)
                a = acc[:, bass.ds((it % B) * QT + t, 1), :].rearrange("p e n -> p (e n)")
                dve.scalar_tensor_tensor(out=a, in0=gen[bank][:, :], scalar=out_scale[:, 0:1], in1=a,
                                         op0=ALU.mult, op1=ALU.add).then_inc(out_added, 1)

            for i in range(len(FIRST)):
                first_low(i)
            expert_out(NS // RING - 1, 2)
            k_low(0, 0)
            q_low(1, 0, 0)
            q_low(2, 1, 1)
            mask_rows(0, 0)
            weights_lo(0, 3, 4, 0)
            first_low(len(FIRST))
            q_low(0, 2, 0)
            mask_rows(1, 1)
            split_hi(0, 0)
            split_lo(0, 0)

            def pair(it, first=False, last=False):
                for r in range(R):
                    n = it * R + r
                    scores = not (last and r >= 2)
                    more = not (last and r == R - 1)
                    if scores:
                        mask_rows(n + 2, r % 2, (0, 1))
                    if more:
                        split_hi(n + 1, (r + 1) % 2)
                    if r == 3 and not first:
                        dve.wait_ge(ffn_added, it + 1)
                        add_out(OUT_BANK[2], it - 1, 2)
                    if r != 3 and not (last and r >= 1):
                        q_low(Q_BANK[r], n + 3, (r + 1) % 2)
                    if scores:
                        mask_rows(n + 2, r % 2, (2,))
                    if r == 0:
                        v_low(V_BANK, it)
                    if r == 3 and first:
                        q_low(Q_BANK[r], n + 3, (r + 1) % 2)
                    if more:
                        split_lo(n + 1, (r + 1) % 2)
                    if r == 0 and first:
                        for i in range(1, len(NEXT)):
                            first_low(len(FIRST) + i)
                    if r == 1 and not last:
                        k_low(K_BANK, it + 1)
                    if r == 3 and not first and not last:
                        q_low(Q_BANK[r], n + 3, (r + 1) % 2)
                    if r == 1 and not first:
                        add_out(OUT_BANK[0], it - 1, 0)
                    if not (first and r == 0):
                        o_low(n - 1, it if r else it - 1, (r - 1) % R)
                    if r == 2 and not first:
                        add_out(OUT_BANK[1], it - 1, 1)
                    if r == 2:
                        add_ffn(it, first)
                    if r == 3 and not last:
                        weights_lo(it + 1, it + 5, it + 5, it + 3)
                    if r == 3 and not first:
                        add_out(OUT_BANK[3], it - 1, 3)

            pair(0, first=True)
            with dve.Fori(1, NIT - 1) as it:
                pair(it)
            pair(NIT - 1, last=True)
            o_low(NH - 1, NIT - 1, R - 1)
            for t in range(QT):
                add_out(TAIL_BANK[t], NIT - 1, t)

        @block.tensor
        def _(pe):
            def products(dst, pairs):
                n = len(pairs)
                for i, (stat, mov) in enumerate(pairs):
                    for m, (a, b) in enumerate(PARTS):
                        ins = pe.matmul(dst, stat(a), mov(b), start=(i == 0 and m == 0),
                                        stop=(i == n - 1 and m == len(PARTS) - 1))
                return ins

            pe.wait_ge(consts, 12)

            GATE_FROM, gated = 6, 0

            def gate(t):
                pe.wait_ge(xt_done, t + 1)
                for k in range(KT):
                    for a in (HI, LO):
                        for b in (HI, LO):
                            ins = pe.matmul(gen[0][:, t * NE:(t + 1) * NE], xt[:, a, k, t * P:(t + 1) * P],
                                            wg[:, b, k, :],
                                            start=(k == 0 and a == HI and b == HI),
                                            stop=(k == KT - 1 and a == LO and b == LO))
                return ins

            for t in range(NT):
                pe.wait_ge(xhi_done, t + 1)
                pe.wait_ge(xlo_done, t + 1)
                if t >= 2:
                    pe.wait_ge(xt_done, t - 1)
                for s in (HI, LO):
                    for k in range(KT):
                        c = (s * KT + k) * P
                        ins = pe.transpose(tra[t % 2][:, c:c + P], xs[:, t % 4, s, k * P:(k + 1) * P], ident[:, :])
                ins.then_inc(xt_filled, 1)
                if t == GATE_FROM:
                    pe.wait_ge(wg_done, 1)
                for _ in range(2 if t >= GATE_FROM else 0):
                    if gated < t:
                        gate(gated)
                        gated += 1
            gate(NT - 1).then_inc(gate_filled, 1)

            pe.wait_ge(chosen_done, 1)
            width = (NT + 1) * NE
            flat = chosen[:, :, :].rearrange("p t e -> p (t e)")
            pe.matmul(gen[1][:, 0:width], before[:, :], flat, start=True, stop=False, skip_group_check=True)
            for t in range(NT):
                ins = pe.matmul(gen[1][:, (t + 1) * NE:width], ones[:, :],
                                chosen[:, t:t + 1, :].broadcast_to([P, NT - t, NE]),
                                start=False, stop=(t == NT - 1), skip_group_check=True)
            ins.then_inc(rank_filled, 1)
            for j in range(TOP * NT):
                pe.wait_ge(hot_done, j + 1)
                pe.matmul(gen[0][:, 0:NS], hot_row[:, j % 4, :], hot_tile[:, j, :], start=(j == 0),
                          stop=(j == TOP * NT - 1)).then_inc(hot_used, 1)

            def slot_rows(u, k):
                i = RING * u + k
                pe.wait_ge(xg_loaded[k], 16 * (u + 1))
                pe.wait_ge(xgT_free, i + 1)
                for c in range(2 * KT):
                    ins = pe.transpose(xbank[k][:, c * P:(c + 1) * P], xg[:, k, c * P:(c + 1) * P], ident[:, :])
                ins.then_inc(xg_filled, 1)

            def expert_product(u, k):
                i = RING * u + k
                e = pe.value_load(expi[0:1, bass.ds(i, 1)], min_val=0, max_val=NE - 1)
                pe.wait_ge(xgT_free, i + 1 + RING)
                pe.wait_ge(ybank_free, i + 1)
                products(ybank[k][:, :],
                         [(lambda a, c=c: xgT[k][:, a, c, :],
                           lambda b, c=c: we[:, bass.ds(e, 1), b, c * D:(c + 1) * D]) for c in range(KT)]
                         ).then_inc(y_filled, 1)

            pe.wait_ge(routed, 1)
            wait_experts(pe)
            slot_rows(0, 0)
            with pe.Fori(0, NS // RING - 1) as u:
                for k in range(RING):
                    slot_rows(u + (k + 1) // RING, (k + 1) % RING)
                    expert_product(u, k)
            for k in range(RING):
                if k + 1 < RING:
                    slot_rows(NS // RING - 1, k + 1)
                expert_product(NS // RING - 1, k)

            def tokens(part, k, it, lo=0, n=S):
                return xt[:, part, k, bass.ds((it % B) * S + lo, n)]

            def fill_q(bank, h, it, r):
                w = bass.ds(((it // B) % 2) * R + r, 1)
                products(gen[bank][:, :], [(lambda a, k=k: wq[:, w, a, k, :], lambda b, k=k: tokens(b, k, it))
                                           for k in range(KT)]).then_inc(q_filled, 1)

            def fill_k(bank, it):
                w = bass.ds((it // B) % 2, 1)
                products(gen[bank][:, :], [(lambda a, k=k: wk[:, w, k, a, :], lambda b, k=k: tokens(b, k, it))
                                           for k in range(KT)]).then_inc(k_filled, 1)

            def fill_v(bank, it):
                w = bass.ds((it // B) % 2, 1)
                products(gen[bank][:, :], [(lambda a, k=k: wv[:, w, k, a, :], lambda b, k=k: tokens(b, k, it))
                                           for k in range(KT)]).then_inc(v_filled, 1)

            def fill_scores(h, slot, fills=(0, 1, 2)):
                if 0 in fills:
                    pe.wait_ge(q_ready, h + 1)
                for u in fills:
                    tiles = SCORE_FILLS[u]
                    if not (isinstance(h, int) and h == 0):
                        pe.wait_ge(s_masked, 3 * h + u - 2)
                    at = 0
                    for i in tiles:
                        w = P * (i + 1)
                        ins = products(sco[u][:, at:at + w],
                                       [(lambda a: qT[:, slot, a, i * P:(i + 1) * P], lambda b: kT[:, b, 0:w])])
                        at += w
                    ins.then_inc(s_filled, 1)

            def fill_o(h, slot):
                pe.wait_ge(pt_ready[slot], 8 * (h - slot + 2))
                if not (isinstance(h, int) and h < 2):
                    pe.wait_ge(o_ready, h - 1)

                def blocks(part, j, lo, n):
                    if n == 1:
                        return pT[:, slot, part, SCORE_AT[lo] + j * P:SCORE_AT[lo] + (j + 1) * P]
                    step = SCORE_AT[lo + 1] - SCORE_AT[lo]
                    rows = pT[:, slot, part, SCORE_AT[lo]:SCORE_AT[lo] + 2 * step].rearrange("p (i c) -> p i c", i=2)
                    return rows[:, :, j * P:(j + 1) * P]

                for j in range(QT):
                    for m, (a, b) in enumerate(PARTS):
                        for lo, n in {0: ((0, 2), (2, 2)), 1: ((1, 1), (2, 2)), 2: ((2, 2),), 3: ((3, 1),)}[j]:
                            ins = pe.matmul(att[slot][:, lo * P:(lo + n) * P], vs[:, a, j, :], blocks(b, j, lo, n),
                                            start=(j == 0 and m == 0 and lo == 0),
                                            stop=(j == lo + n - 1 and m == len(PARTS) - 1),
                                            skip_group_check=True)
                ins.then_inc(o_filled, 1)

            def fill_out(bank, it, t):
                if t == 0:
                    pe.wait_ge(o_ready, R * it + R)
                w = (it // B) % 2
                products(gen[bank][:, :],
                         [(lambda a, r=r: oT[:, bass.ds(it % 2, 1), r, a, t * P:(t + 1) * P],
                           lambda b, r=r: wo[:, bass.ds(w * R + r, 1), b, :]) for r in range(R)]).then_inc(out_filled, 1)

            pe.wait_ge(first_ready, 1)
            fill_k(0, 0)
            pe.wait_ge(first_ready, 2)
            fill_q(1, 0, 0, 0)
            pe.wait_ge(first_ready, 3)
            fill_q(2, 1, 0, 1)
            pe.wait_ge(k_ready, 1)
            pe.wait_ge(ybank_free, NS + RING)
            fill_scores(0, 0)
            pe.wait_ge(first_ready, 5)
            fill_q(0, 2, 0, 2)
            fill_scores(1, 1)
            def pair(it, first=False, last=False):
                for r in range(R):
                    n = it * R + r
                    if r == 2 and not last:
                        pe.wait_ge(k_ready, it + 2)
                    if not (last and r >= 2):
                        fill_scores(n + 2, r % 2, (0, 1))
                    if r == 1:
                        if first:
                            pe.wait_ge(first_ready, len(FIRST) + 1)
                        else:
                            pe.wait_ge(w_ready, it + 1)
                    if r == 3 and not first:
                        pe.wait_ge(out_added, QT * (it - 1) + 1)
                        fill_out(OUT_BANK[2], it - 1, 2)
                    if r == 0 and first:
                        pe.wait_ge(w_ready, 1)
                    if r != 3 and not (last and r >= 1):
                        fill_q(Q_BANK[r], n + 3, it + (r > 0), (r + 3) % R)
                    if r == 0:
                        if not first:
                            pe.wait_ge(s_masked, 3 * (n + 2) + 1)
                        fill_v(V_BANK, it)
                    if not (last and r >= 2):
                        fill_scores(n + 2, r % 2, (2,))
                    if r == 1 and not last:
                        fill_k(K_BANK, it + 1)
                    if r == 3 and not last:
                        fill_q(Q_BANK[r], n + 3, it + 1, (r + 3) % R)
                    if r == 3 and first:
                        pe.wait_ge(first_ready, len(FIRST) + len(NEXT))
                    if r == 1:
                        if not first:
                            pe.wait_ge(v_ready, it + 1)
                            fill_out(OUT_BANK[0], it - 1, 0)
                        pe.wait_ge(vs_ready, 16 * (it + 1))
                    if not (first and r == 0):
                        fill_o(n - 1, (r + 1) % 2)
                    if r == 2 and not first:
                        fill_out(OUT_BANK[1], it - 1, 1)
                    if r == 3 and not first:
                        pe.wait_ge(out_added, QT * (it - 1) + 3)
                        fill_out(OUT_BANK[3], it - 1, 3)

            pair(0, first=True)
            with pe.Fori(1, NIT - 1) as it:
                pair(it)
            pair(NIT - 1, last=True)
            fill_o(NH - 1, 1)
            for t in range(QT):
                if t >= 2:
                    pe.wait_ge(out_added, QT * (NIT - 1) + t - 2)
                fill_out(TAIL_BANK[t], NIT - 1, t)


Q_BANK = (0, 2, 2, 2)
K_BANK = 0
V_BANK = 1
OUT_BANK = (1, 0, 1, 1)
TAIL_BANK = (2, 0, 1, 2)


_INS = ['L0_attn_hidden_states', 'L0_attn_w_q', 'L0_attn_w_k', 'L0_attn_w_v', 'L0_attn_w_o', 'L0_ffn_W_gate',
        'L0_ffn_b_gate', 'L0_ffn_W_e', 'L0_ffn_b_e']


def kernel(**inputs):
    import numpy as _np
    import concourse.bacc as _bacc
    from concourse import mybir as _mybir
    from concourse.bass_utils import run_bass_kernel_spmd as _run

    nc = _bacc.Bacc("TRN2", target_bir_lowering=False, num_devices=1)
    arrays, args = {}, []
    for name in _INS:
        a = _np.ascontiguousarray(inputs[name])
        arrays[f"in_{name}_dram"] = a
        args.append(nc.dram_tensor(f"in_{name}_dram", a.shape, _mybir.dt.from_np(a.dtype), kind="ExternalInput").ap())
    shape = inputs[_INS[0]].shape
    args.append(nc.dram_tensor("out_0_dram", shape, F32, kind="ExternalOutput").ap())
    attention_moe(nc, *args)
    r = _run(nc, [arrays], core_ids=[0])
    return r.results[0]["out_0_dram"]
```
